# Optimizing a Trainium2 kernel written in Bass

```python
import numpy as np
import jax
import jax.numpy as jnp

def _softmax(x, axis=-1):
    return jax.nn.softmax(x, axis=axis)

def _gelu(x):
    return jax.nn.gelu(x, approximate=True)

def _silu(x):
    return jax.nn.silu(x)

def _sigmoid(x):
    return jax.nn.sigmoid(x)

def _layernorm(x, axis=-1, eps=1e-05):
    m = jnp.mean(x, axis=axis, keepdims=True)
    v = jnp.var(x, axis=axis, keepdims=True)
    return (x - m) / jnp.sqrt(v + eps)

def _scatter_add(tgt, idx, src, axis=0):
    return tgt.at[idx].add(src)

def _segment_sum(src, seg, n):
    return jax.ops.segment_sum(src, seg, n)
kernel_name = 'mk_flamingo_gated_d1_seqx_r4_356c52'

def setup_inputs(seed: int=0):
    np.random.seed(seed)
    _w = jnp.asarray

    def _rec_inputs():
        import jax
        import jax.numpy as jnp
        _rk = jax.random.key(seed)
        x = -0.000125 + 0.9999 * jax.random.normal(jax.random.fold_in(_rk, 1), (32, 128, 512), jnp.float32)
        _lenS = 128 - jax.random.randint(jax.random.fold_in(_rk, 7), (32,), 0, max(1, 128 // 4) + 1, jnp.int32)
        _lenS2 = 128 - jax.random.randint(jax.random.fold_in(_rk, 8), (32,), 0, max(1, 128 // 4) + 1, jnp.int32)
        _ctx_2048P = jax.random.normal(jax.random.fold_in(_rk, 11), (32, 16, 512), jnp.float32)
        _ctx_2048c = jax.random.dirichlet(jax.random.fold_in(_rk, 511), 0.3 * jnp.ones((16,), jnp.float32), (32, 128))
        _ctx_2048t = jnp.einsum('bsk,bkd->bsd', _ctx_2048c, _ctx_2048P)
        _ctx_2048t = _ctx_2048t * jax.lax.rsqrt(jnp.mean(jnp.square(_ctx_2048t)) + 1e-12) * 0.953939
        ctx_2048 = 1.72703e-05 + 1.00003 * (_ctx_2048t + 0.3 * jax.random.normal(jax.random.fold_in(_rk, 611), (32, 128, 512), jnp.float32))
        _g = jax.random.normal(jax.random.fold_in(_rk, 9001), (2, 1), jnp.float32)
        _g = jnp.sign(_g) * jnp.maximum(jnp.abs(_g), 1.0) + (_g == 0) * 1.0
        g_xattn = _g[0]
        g_ffn = _g[1]
        return (x, ctx_2048, g_xattn, g_ffn)
    x, ctx_2048, g_xattn, g_ffn = _rec_inputs()

    def _L0_xattn_setup():
        import jax, jax.numpy as jnp
        import numpy as np
        DIM = 512
        NH = 16
        HD = DIM // NH
        EPS = 1e-06
        IMG_LEN = 257

        def rms_norm(x, w, eps=EPS):
            xf = x.astype(jnp.float32)
            y = xf * jax.lax.rsqrt(jnp.mean(xf * xf, axis=-1, keepdims=True) + eps)
            return y.astype(x.dtype) * w

        def linear(x, w, b):
            return jnp.einsum('blc,oc->blo', x, w) + b

        def attention(q, k, v):
            scale = 1.0 / jnp.sqrt(jnp.asarray(HD, q.dtype))
            scores = jnp.einsum('bqhd,bkhd->bhqk', q, k) * scale
            probs = jax.nn.softmax(scores, axis=-1)
            return jnp.einsum('bhqk,bkhd->bqhd', probs, v)
        key = jax.random.key(seed)
        ks = jax.random.split(key, 12)
        B, L = (2, 2048)
        s = 0.02
        inp = {'x': jax.random.normal(ks[0], (B, L, DIM), jnp.float32), 'context': jax.random.normal(ks[1], (B, 769, DIM), jnp.float32), 'q_w': jax.random.normal(ks[2], (DIM, DIM), jnp.float32) * s, 'q_b': jnp.zeros((DIM,), jnp.float32), 'k_w': jax.random.normal(ks[3], (DIM, DIM), jnp.float32) * s, 'k_b': jnp.zeros((DIM,), jnp.float32), 'v_w': jax.random.normal(ks[4], (DIM, DIM), jnp.float32) * s, 'v_b': jnp.zeros((DIM,), jnp.float32), 'k_img_w': jax.random.normal(ks[5], (DIM, DIM), jnp.float32) * s, 'k_img_b': jnp.zeros((DIM,), jnp.float32), 'v_img_w': jax.random.normal(ks[6], (DIM, DIM), jnp.float32) * s, 'v_img_b': jnp.zeros((DIM,), jnp.float32), 'o_w': jax.random.normal(ks[7], (DIM, DIM), jnp.float32) * s, 'o_b': jnp.zeros((DIM,), jnp.float32), 'norm_q_w': jnp.ones((DIM,), jnp.float32), 'norm_k_w': jnp.ones((DIM,), jnp.float32), 'norm_k_img_w': jnp.ones((DIM,), jnp.float32)}
        return inp
    _L0_xattn_all = _L0_xattn_setup()
    _L0_xattn_in = {k: v for k, v in _L0_xattn_all.items() if k in ('q_w', 'q_b', 'k_w', 'k_b', 'v_w', 'v_b', 'k_img_w', 'k_img_b', 'v_img_w', 'v_img_b', 'o_w', 'o_b', 'norm_q_w', 'norm_k_w', 'norm_k_img_w')}
    del _L0_xattn_all

    def _L0_ffn_setup():
        import jax, jax.numpy as jnp
        import numpy as np
        DIM = 512
        HIDDEN = 2048
        GROUP = 64

        def _ternary_weight(w, group_size):
            wb = w.astype(jnp.bfloat16)
            wg = wb.reshape(-1, group_size)
            scale = jnp.clip(jnp.mean(jnp.abs(wg), axis=-1, keepdims=True), 1e-08, None)
            q = jnp.clip(jnp.round(wg / scale), -1.0, 1.0)
            qs = (q * scale).reshape(w.shape).astype(w.dtype)
            return w + jax.lax.stop_gradient(qs - w)

        def _rms_norm(x):
            eps = jnp.asarray(jnp.finfo(x.dtype).eps, x.dtype)
            ms = jnp.mean(jnp.square(x), axis=-1, keepdims=True)
            return x * jax.lax.rsqrt(ms + eps)
        key = jax.random.key(seed)
        k_x, k_fc, k_proj = jax.random.split(key, 3)
        x = jax.random.normal(k_x, (4, 1024, DIM), dtype=jnp.float32)
        W_fc = jax.random.normal(k_fc, (HIDDEN, DIM), dtype=jnp.float32) / np.sqrt(DIM)
        W_proj = jax.random.normal(k_proj, (DIM, HIDDEN), dtype=jnp.float32) / np.sqrt(HIDDEN)
        return {'x': x, 'W_fc': W_fc, 'W_proj': W_proj}
    _L0_ffn_all = _L0_ffn_setup()
    _L0_ffn_in = {k: v for k, v in _L0_ffn_all.items() if k in ('W_fc', 'W_proj')}
    del _L0_ffn_all
    return {'x': x, 'ctx_2048': ctx_2048, 'g_xattn': g_xattn, 'g_ffn': g_ffn, 'L0_xattn_q_w': _L0_xattn_in['q_w'], 'L0_xattn_q_b': _L0_xattn_in['q_b'], 'L0_xattn_k_w': _L0_xattn_in['k_w'], 'L0_xattn_k_b': _L0_xattn_in['k_b'], 'L0_xattn_v_w': _L0_xattn_in['v_w'], 'L0_xattn_v_b': _L0_xattn_in['v_b'], 'L0_xattn_k_img_w': _L0_xattn_in['k_img_w'], 'L0_xattn_k_img_b': _L0_xattn_in['k_img_b'], 'L0_xattn_v_img_w': _L0_xattn_in['v_img_w'], 'L0_xattn_v_img_b': _L0_xattn_in['v_img_b'], 'L0_xattn_o_w': _L0_xattn_in['o_w'], 'L0_xattn_o_b': _L0_xattn_in['o_b'], 'L0_xattn_norm_q_w': _L0_xattn_in['norm_q_w'], 'L0_xattn_norm_k_w': _L0_xattn_in['norm_k_w'], 'L0_xattn_norm_k_img_w': _L0_xattn_in['norm_k_img_w'], 'L0_ffn_W_fc': _L0_ffn_in['W_fc'], 'L0_ffn_W_proj': _L0_ffn_in['W_proj']}

def reference(x, ctx_2048, g_xattn, g_ffn, L0_xattn_q_w, L0_xattn_q_b, L0_xattn_k_w, L0_xattn_k_b, L0_xattn_v_w, L0_xattn_v_b, L0_xattn_k_img_w, L0_xattn_k_img_b, L0_xattn_v_img_w, L0_xattn_v_img_b, L0_xattn_o_w, L0_xattn_o_b, L0_xattn_norm_q_w, L0_xattn_norm_k_w, L0_xattn_norm_k_img_w, L0_ffn_W_fc, L0_ffn_W_proj):
    import jax
    import jax.numpy as jnp

    def _L0_xattn_ref(x, context, q_w, q_b, k_w, k_b, v_w, v_b, k_img_w, k_img_b, v_img_w, v_img_b, o_w, o_b, norm_q_w, norm_k_w, norm_k_img_w):
        import jax, jax.numpy as jnp
        import numpy as np
        DIM = 512
        NH = 16
        HD = DIM // NH
        EPS = 1e-06
        IMG_LEN = 257

        def rms_norm(x, w, eps=EPS):
            xf = x.astype(jnp.float32)
            y = xf * jax.lax.rsqrt(jnp.mean(xf * xf, axis=-1, keepdims=True) + eps)
            return y.astype(x.dtype) * w

        def linear(x, w, b):
            return jnp.einsum('blc,oc->blo', x, w) + b

        def attention(q, k, v):
            scale = 1.0 / jnp.sqrt(jnp.asarray(HD, q.dtype))
            scores = jnp.einsum('bqhd,bkhd->bhqk', q, k) * scale
            probs = jax.nn.softmax(scores, axis=-1)
            return jnp.einsum('bhqk,bkhd->bqhd', probs, v)
        B, L, _ = x.shape
        ctx_img = context[:, :IMG_LEN]
        ctx_txt = context[:, IMG_LEN:]
        q = rms_norm(linear(x, q_w, q_b), norm_q_w).reshape(B, L, NH, HD)
        k = rms_norm(linear(ctx_txt, k_w, k_b), norm_k_w).reshape(B, -1, NH, HD)
        v = linear(ctx_txt, v_w, v_b).reshape(B, -1, NH, HD)
        k_img = rms_norm(linear(ctx_img, k_img_w, k_img_b), norm_k_img_w).reshape(B, -1, NH, HD)
        v_img = linear(ctx_img, v_img_w, v_img_b).reshape(B, -1, NH, HD)
        img_x = attention(q, k_img, v_img)
        txt_x = attention(q, k, v)
        out = (txt_x + img_x).reshape(B, L, DIM)
        return linear(out, o_w, o_b)

    def _L0_ffn_ref(x, W_fc, W_proj):
        import jax, jax.numpy as jnp
        import numpy as np
        DIM = 512
        HIDDEN = 2048
        GROUP = 64

        def _ternary_weight(w, group_size):
            wb = w.astype(jnp.bfloat16)
            wg = wb.reshape(-1, group_size)
            scale = jnp.clip(jnp.mean(jnp.abs(wg), axis=-1, keepdims=True), 1e-08, None)
            q = jnp.clip(jnp.round(wg / scale), -1.0, 1.0)
            qs = (q * scale).reshape(w.shape).astype(w.dtype)
            return w + jax.lax.stop_gradient(qs - w)

        def _rms_norm(x):
            eps = jnp.asarray(jnp.finfo(x.dtype).eps, x.dtype)
            ms = jnp.mean(jnp.square(x), axis=-1, keepdims=True)
            return x * jax.lax.rsqrt(ms + eps)
        w1 = _ternary_weight(W_fc, GROUP)
        h = jnp.einsum('bsd,hd->bsh', x, w1)
        h = jnp.square(jax.nn.relu(h))
        hn = _rms_norm(h)
        w2 = _ternary_weight(W_proj, GROUP)
        return jnp.einsum('bsh,dh->bsd', hn, w2)
    x = x + jnp.tanh(g_xattn[0]) * _L0_xattn_ref(_layernorm(x, axis=-1), ctx_2048, L0_xattn_q_w, L0_xattn_q_b, L0_xattn_k_w, L0_xattn_k_b, L0_xattn_v_w, L0_xattn_v_b, L0_xattn_k_img_w, L0_xattn_k_img_b, L0_xattn_v_img_w, L0_xattn_v_img_b, L0_xattn_o_w, L0_xattn_o_b, L0_xattn_norm_q_w, L0_xattn_norm_k_w, L0_xattn_norm_k_img_w)
    x = x + jnp.tanh(g_ffn[0]) * _L0_ffn_ref(_layernorm(x, axis=-1), L0_ffn_W_fc, L0_ffn_W_proj)
    return x

_drawn_inputs = setup_inputs


def setup_inputs(seed=0):
    import zlib

    import numpy as np

    out = dict(_drawn_inputs(seed))
    spreads = {'L0_xattn_q_b': (0.0, 0.1),
     'L0_xattn_k_b': (0.0, 0.1),
     'L0_xattn_v_b': (0.0, 0.1),
     'L0_xattn_k_img_b': (0.0, 0.1),
     'L0_xattn_v_img_b': (0.0, 0.1),
     'L0_xattn_o_b': (0.0, 0.1),
     'L0_xattn_norm_q_w': (1.0, 0.2),
     'L0_xattn_norm_k_w': (1.0, 0.2),
     'L0_xattn_norm_k_img_w': (1.0, 0.2)}
    factors = {}
    for name, (base, spread) in spreads.items():
        noise = np.random.default_rng([zlib.crc32(name.encode()), seed]).standard_normal(out[name].shape)
        drawn = base * np.exp(spread * noise) if base else spread * noise
        out[name] = jnp.asarray(drawn.astype(out[name].dtype))
    for name, factor in factors.items():
        out[name] = (out[name] * factor).astype(out[name].dtype)
    return out
```

```python
from contextlib import ExitStack

import concourse.bass as bass
from concourse import mybir

F32 = mybir.dt.float32
F16 = mybir.dt.float16
BF16 = mybir.dt.bfloat16
ALU = mybir.AluOpType
ACT = mybir.ActivationFunctionType
AX = mybir.AxisListType
RMAX = bass.bass_isa.ReduceOp.max

P = 128
LN_EPS = 1e-5
QK_EPS = 1e-6
FFN_EPS = 2.0 ** -23
TINY = 1e-30
GROUP = 64
TERNARY_CLIP = 1.001171767711639404296875e-08

X_SCALE = 2.0 ** 10
W_MAX = 2.0 ** 10
C_MAX = 2.0 ** 14
QK_SCALE = 2.0 ** 10
V_SCALE = 2.0 ** -18
LOG_P_SCALE = 9.70406052783923
R_MAX = 181.0


def gated_cross_attention_kernel(nc, x, ctx_t, gains, wq_t, wk_t, wv_t, wo_t, q_b, k_b, o_b, norm_q, norm_k, v_b,
                                 w_fc_t, w_proj_t, out):
    NT = x.shape[0]
    D = x.shape[2]
    C = D // P
    HID = w_fc_t.shape[2]
    M = HID // P
    HD = 32
    H = D // HD
    J = 4
    NG = NT // J
    R = 2 * P
    UP = 4
    LAG = 4
    NU = HID * D // (P * 512)
    TERN = 8
    TD = 5
    TABS = 6
    TAHEAD = 4
    assert C == 4 and M == 4 * UP and H == 16 and NT % J == 0 and J * TERN == 2 * NU

    stack = ExitStack()
    with stack:
        def sb(name, shape, dt=F32):
            return stack.enter_context(nc.sbuf_tensor(name, shape, dt))

        def sem(name):
            return stack.enter_context(nc.semaphore(name))

        def sems(name, n):
            return [sem(f"{name}{i}") for i in range(n)]

        banks = [stack.enter_context(nc.psum_tensor(f"bank{i}", [P, 512], F32)) for i in range(8)]
        score_ps = banks[0:4]
        q_ps, k_ps, v_ps, o_ps = score_ps
        up_ps = banks[4]
        mix_ps = banks[5]
        tr_a, tr_b = banks[6:8]

        ident = sb("ident", [P, P])
        ones_col = sb("ones_col", [P, 1])
        minus_half = sb("minus_half", [P, 2])
        group_ones = sb("group_ones", [P, P], BF16)
        gain_in = sb("gain_in", [P, 2])
        gain = sb("gain", [P, 2])
        w_hi = [sb(f"w{n}_hi", [P, C, D], F16) for n in "qkvo"]
        w_lo = [sb(f"w{n}_lo", [P, C, D], F16) for n in "qkvo"]
        w_top = sb("w_top", [P, 4])
        w_top_all = sb("w_top_all", [P, 4])
        w_step = sb("w_step", [P, 4])
        w_scale = sb("w_scale", [P, 4])
        w1 = sb("w1", [P, C, HID], BF16)
        w2 = sb("w2", [P, M, D], BF16)
        qb_sb = sb("qb_sb", [P, D])
        kb_sb = sb("kb_sb", [P, D])
        qk_norm = sb("qk_norm", [P, D])
        o_const = sb("o_const", [P, D])
        vb_col = sb("vb_col", [P, C])
        qk_top = sb("qk_top", [P, 1])
        qk_inv = sb("qk_inv", [P, 1])
        exp_scale = sb("exp_scale", [P, 1])
        neg_exp_scale = sb("neg_exp_scale", [P, 1])
        q_unscale = sb("q_unscale", [P, 1])
        k_unscale0 = sb("k_unscale0", [P, 1])
        o_unscale0 = sb("o_unscale0", [P, 1])
        scale_top = sb("scale_top", [P, 512], BF16)
        fc_top = sb("fc_top", [P, 1])
        fc_top_all = sb("fc_top_all", [P, 1])
        relu_scale = sb("relu_scale", [P, 1])
        h_unscale = sb("h_unscale", [P, 1])
        ms_scale = sb("ms_scale", [P, 1])
        out_gain = sb("out_gain", [P, 1])
        tmp_c = sb("tmp_c", [P, 4])

        x_sb = [sb(f"x_sb{i}", [P, D]) for i in range(4)]
        ctx_sb = [sb(f"ctx_sb{i}", [P, D]) for i in range(2)]
        ln1_raw = sb("ln1_raw", [P, 6])
        ln1_mv = sb("ln1_mv", [P, 2])
        ln1_in = sb("ln1_in", [P, 2])
        ln1_rstd = sb("ln1_rstd", [P, 1])
        xn = sb("xn", [P, D])
        xt_hi = sb("xt_hi", [P, D], F16)
        xt_lo = sb("xt_lo", [P, D], F16)
        ctx_part = sb("ctx_part", [P, 1])
        ctx_top = sb("ctx_top", [P, 1])
        ctx_step = sb("ctx_step", [P, 1])
        ctx_scale = sb("ctx_scale", [P, 1])
        k_unscale = sb("k_unscale", [P, 1])
        o_unscale = [sb(f"o_unscale_t{i}", [P, 1]) for i in range(2)]
        ct_hi = sb("ct_hi", [P, D], F16)
        ct_lo = sb("ct_lo", [P, D], F16)
        q_raw = sb("q_raw", [P, D])
        k_raw = sb("k_raw", [P, D])
        square_out = [sb(f"square_out{i}", [P, D], BF16) for i in range(2)]
        q_ss = sb("q_ss", [P, 1])
        k_ss = sb("k_ss", [P, 1])
        q_ms = sb("q_ms", [P, 1])
        k_ms = sb("k_ms", [P, 1])
        q_rms = sb("q_rms", [P, 1])
        k_rms = sb("k_rms", [P, 1])
        qn = sb("qn", [P, D])
        kn = sb("kn", [P, D])
        qt_hi = sb("qt_hi", [P, D], F16)
        qt_lo = sb("qt_lo", [P, D], F16)
        kt_hi = sb("kt_hi", [P, D], F16)
        kt_lo = sb("kt_lo", [P, D], F16)
        v_hi = sb("v_hi", [P, D], F16)
        v_lo = sb("v_lo", [P, D], F16)
        s_top = sb("s_top", [P, H])
        exp_bias = sb("exp_bias", [P, H])
        p_sum = sb("p_sum", [P, H])
        p_inv = sb("p_inv", [P, H])
        p_sb = [sb(f"p_sb{i}", [P, 512]) for i in range(4)]
        pt_hi = [sb(f"pt_hi{i}", [P, 512], F16) for i in range(2)]
        pt_lo = [sb(f"pt_lo{i}", [P, 512], F16) for i in range(2)]
        attn = sb("attn", [P, D])
        at_hi = sb("at_hi", [P, D], F16)
        at_lo = sb("at_lo", [P, D], F16)
        xb = sb("xb", [P, D])
        x1 = [sb(f"x1_{j}", [P, D]) for j in range(LAG)]
        ln2_raw = sb("ln2_raw", [P, 6])
        ln2_mv = sb("ln2_mv", [P, 2])
        ln2_in = sb("ln2_in", [P, 2])
        ln2_rstd = sb("ln2_rstd", [P, 1])
        x1n = sb("x1n", [P, D])
        ft_hi = [sb(f"ft_hi{i}", [P, C, R], F16) for i in range(2)]
        ft_lo = [sb(f"ft_lo{i}", [P, C, R], F16) for i in range(2)]
        relu_sb = [sb(f"relu_sb{i}", [P, 512]) for i in range(2)]
        h_sb = [sb(f"h_sb{i}", [P, 512]) for i in range(2)]
        hh_sb = [sb(f"hh_sb{i}", [P, 512]) for i in range(2)]
        hh_sum = sb("hh_sum", [P, 512])
        h_ms = sb("h_ms", [P, 2])
        h_rms = sb("h_rms", [P, 2])
        h_gain = sb("h_gain", [P, 2])
        out_sb = [sb(f"out_sb{i}", [P, D]) for i in range(2)]
        big = sb("big", [P, 4 * C * 512])
        stage = [big[:, s * 2048:(s + 1) * 2048] for s in range(4)]
        ht_hi, ht_lo = ([big[:, o + 4096 * i:o + 4096 * i + 2048].bitcast(F16) for i in range(2)] for o in (0, 2048))
        before_out = [out_sb[i // 2][:, i % 2 * 256:(i % 2 + 1) * 256].bitcast(BF16) for i in range(4)]
        abs_w = [sb(f"abs_w{i}", [P, 512], BF16)[:, :] for i in range(TABS - 2)] + before_out[0:2]
        t_scale = [sb(f"t_scale{i}", [P, 512], BF16)[:, :] for i in range(TD - 1)] + before_out[2:3]
        t_mask = [sb(f"t_mask{i}", [P, 512], BF16)[:, :] for i in range(TD - 1)] + before_out[3:4]
        vb_wide = x1[0][:, :].rearrange("p (c k) -> p c k", c=C)
        ob_in = x1[1]
        nk_in = x1[2]

        consts_ready = sem("consts_ready")
        zeros_ready = sem("zeros_ready")
        small_in = sem("small_in")
        stage_in = sems("stage_in", 4)
        w_top_part, w_top_spread, w_top_ready, w_scale_ready, w_hi_ready = (
            sem(n) for n in ("w_top_part", "w_top_spread", "w_top_ready", "w_scale_ready", "w_hi_ready"))
        w_lo_ready = sems("w_lo_ready", 4)
        w_step_ready = sem("w_step_ready")
        gain_ready, vb_ready, wov_done, setup_dve = (sem(n) for n in ("gain_ready", "vb_ready", "wov_done", "setup_dve"))
        abs_ready, sign_ready, gsum_done, tscale_ready, tmax_ready, tmask_ready, tsigned_ready, tern_ready = (
            sem(n) for n in ("abs_ready", "sign_ready", "gsum_done", "tscale_ready", "tmax_ready", "tmask_ready",
                             "tsigned_ready", "tern_ready"))
        fc_top_part, fc_top_spread, ffn_consts = (sem(n) for n in ("fc_top_part", "fc_top_spread", "ffn_consts"))
        x_in = sems("x_in", 4)
        ctx_in = sems("ctx_in", 2)
        out_free = sems("out_free", 2)
        dve_step = sem("dve_step")
        ln1_ready, ln1_rstd_ready, xn_ready, xt_done, xhi_ready, xlo_ready = (
            sem(n) for n in ("ln1_ready", "ln1_rstd_ready", "xn_ready", "xt_done", "xhi_ready", "xlo_ready"))
        ctx_part_ready, ctx_spread, ctx_top_ready, ctx_step_ready, ctx_scale_ready, chi_ready, clo_ready = (
            sem(n) for n in ("ctx_part_ready", "ctx_spread", "ctx_top_ready", "ctx_step_ready", "ctx_scale_ready",
                             "chi_ready", "clo_ready"))
        q_done, k_done, v_done, o_done = (sem(n) for n in ("q_done", "k_done", "v_done", "o_done"))
        qraw_ready, kraw_ready, qss_ready, kss_ready = (
            sem(n) for n in ("qraw_ready", "kraw_ready", "qss_ready", "kss_ready"))
        qms_ready, qrms_ready, qn_ready, kms_ready, krms_ready, kn_ready = (
            sem(n) for n in ("qms_ready", "qrms_ready", "qn_ready", "kms_ready", "krms_ready", "kn_ready"))
        qt_done, kt_done, qhi_ready, qlo_ready, khi_ready, klo_ready, vhi_ready, vlo_ready = (
            sem(n) for n in ("qt_done", "kt_done", "qhi_ready", "qlo_ready", "khi_ready", "klo_ready", "vhi_ready",
                             "vlo_ready"))
        s_done = sem("s_done")
        top_ready, bias_ready, exp_ready, pt_done, phi_ready, plo_ready, pv_done = (
            sem(n) for n in ("top_ready", "bias_ready", "exp_ready", "pt_done", "phi_ready", "plo_ready", "pv_done"))
        pinv_ready, attn_ready, at_done, ahi_ready, alo_ready = (
            sem(n) for n in ("pinv_ready", "attn_ready", "at_done", "ahi_ready", "alo_ready"))
        xb_ready, x1_ready, ln2_ready, ln2_rstd_ready, x1n_ready, ft_done, fhi_ready, flo_ready = (
            sem(n) for n in ("xb_ready", "x1_ready", "ln2_ready", "ln2_rstd_ready", "x1n_ready", "ft_done", "fhi_ready",
                             "flo_ready"))
        up_done, relu_ready, hhi_ready, h_ready, hlo_ready, hh_ready, hsum_ready = (
            sem(n) for n in ("up_done", "relu_ready", "hhi_ready", "h_ready", "hlo_ready", "hh_ready", "hsum_ready"))
        hms_ready, hrms_ready, hgain_ready = (sem(n) for n in ("hms_ready", "hrms_ready", "hgain_ready"))
        hss_done = sem("hss_done")
        down_done, out_ready = (sem(n) for n in ("down_done", "out_ready"))

        block = stack.enter_context(nc.Block())

        def need(eng, s, n):
            if not isinstance(n, int) or n > 0:
                eng.wait_ge(s, n)

        def held(eng, n):
            if not isinstance(n, int):
                eng.compute_val(n)
            return n

        def piece(t, f):
            return UP * t - 2 * UP + f

        def pairs_before(g, j):
            return 2 * g + j // 2 - 1

        def last_slot(t):
            return isinstance(t, int) and t == NT - 1

        def units(t, place, tern):
            if not tern:
                return ()
            here = (place,) if t < 2 else (2 * place, 2 * place + 1) if place < 4 else ()
            return [TERN * t + n for n in here]

        def ternary_place(n):
            if n < NU:
                return w1[:, n // 4, (n % 4) * 512:(n % 4 + 1) * 512]
            return w2[:, n - NU, :]

        def ternary_stage(b):
            return (b, 2) if b < 4 else (2 + b % 2, 3 + (b - 4) // 2)

        @block.sync
        def _(sp):
            def load_tile(t, b):
                need(sp, xb_ready, t - 3)
                sp.dma_start(x_sb[b][:, :], x[bass.ds(t, 1), :, :]).then_inc(x_in[b], 16)
                need(sp, clo_ready, t - 1)
                sp.dma_start(ctx_sb[b % 2][:, :], ctx_t[bass.ds(t, 1), :, :]).then_inc(ctx_in[b % 2], 16)

            def load_ternary(b):
                if b < 4:
                    sp.wait_ge(w_lo_ready[b], 1)
                    if b == 3:
                        sp.wait_ge(wov_done, 1)
                else:
                    sp.wait_ge(sign_ready, 4 * (b - 2) + 4)
                s = ternary_stage(b)[0]
                src = w_fc_t[:, b, :] if b < 4 else w_proj_t[:, (b - 4) * 4:(b - 3) * 4, :]
                sp.dma_start(stage[s], src).then_inc(stage_in[s], 16)

            def store(t, i):
                sp.wait_ge(out_ready, t + 1)
                sp.dma_start(out[bass.ds(t, 1), :, :], out_sb[i % 2][:, :]).then_inc(out_free[i % 2], 16)

            sp.dma_start(x_sb[0][:, :], x[0:1, :, :]).then_inc(x_in[0], 16)
            sp.dma_start(ctx_sb[0][:, :], ctx_t[0:1, :, :]).then_inc(ctx_in[0], 16)
            for s, w in enumerate((wq_t, wk_t, wv_t, wo_t)):
                sp.dma_start(stage[s], w).then_inc(stage_in[s], 16)
                if s == 1:
                    for dst, src in ((gain_in, gains), (qb_sb, q_b), (kb_sb, k_b), (qk_norm, norm_q), (nk_in, norm_k),
                                     (ob_in, o_b), (vb_col, v_b)):
                        sp.dma_start(dst[:, :], src).then_inc(small_in, 16)
            load_tile(1, 1)
            for b in range(4):
                load_ternary(b)
            for t in (2, 3, 4):
                load_tile(t, t % 4)
            load_ternary(4)
            load_ternary(5)
            load_tile(5, 1)
            load_ternary(6)
            load_ternary(7)
            load_tile(6, 2)

            def round_of(g):
                for j in range(J):
                    t = J * g + j
                    if not isinstance(t, int) or t + 3 < NT:
                        load_tile(t + 3, (j + 3) % 4)
                    store(t - LAG, j)

            with sp.Fori(1, NG - 1) as g:
                round_of(g)
            round_of(NG - 1)
            for i in range(LAG):
                store(NT - LAG + i, i)
            for i in range(2):
                sp.wait_ge(out_free[i], 16 * (NT // 2 + 1))

        @block.tensor
        def _(pe):
            def transpose4(dst, src, done):
                for c in range(C):
                    last = nc.tensor.transpose(dst[:, c * P:(c + 1) * P], src[:, c * P:(c + 1) * P], ident[:, :])
                last.then_inc(done, 1)

            def project(dst, hi, lo, w, done):
                for c in range(C):
                    col = slice(c * P, (c + 1) * P)
                    nc.tensor.matmul(dst[:, :], hi[:, col], w_hi[w][:, c, :], start=(c == 0), stop=False)
                    nc.tensor.matmul(dst[:, :], hi[:, col], w_lo[w][:, c, :], start=False, stop=False)
                    last = nc.tensor.matmul(dst[:, :], lo[:, col], w_hi[w][:, c, :], start=False, stop=(c == C - 1))
                last.then_inc(done, 1)

            def spread(dst, column, done):
                nc.tensor.matmul(dst[:, 0:P], column.to_broadcast([P, P]), ident[:, :], start=True,
                                 stop=True).then_inc(done, 1)

            def ffn_up(g, j, f, dst, banks=1):
                t, i, n = J * g + j, (j // 2 + 1) % 2, UP * (j % 2) + f
                if n == 0:
                    pe.wait_ge(flo_ready, t)
                    need(pe, hms_ready, pairs_before(g, j))
                need(pe, relu_ready, piece(t, f) - banks + 1)
                for u in range(2):
                    m = 2 * n + u
                    half = slice(u * R, (u + 1) * R)
                    for c in range(C):
                        w = w1[:, c, m * P:(m + 1) * P]
                        nc.tensor.matmul(dst[:, half], w, ft_hi[i][:, c, :], start=(c == 0), stop=False)
                        last = nc.tensor.matmul(dst[:, half], w, ft_lo[i][:, c, :], start=False, stop=(c == C - 1))
                last.then_inc(up_done, 1)

            def ffn_down(g, j, p, dst, waits=1):
                i, sums = j // 2, j % 2 == 0 and p == (3 if waits == 4 else 1)
                if j % 2 == 0 and (p == 0 or waits == 4):
                    n = 2 * (3 - p) if waits == 4 else 0
                    pe.wait_ge(hlo_ready, piece(J * g + j, 0) - n)
                if sums:
                    pe.wait_ge(hsum_ready, (2 * UP - 1) * pairs_before(g, j))
                    pe.wait_ge(relu_ready, piece(J * g + j, 0))
                for m in range(4 * p, 4 * p + 4):
                    row = slice(m * R + j % 2 * P, m * R + j % 2 * P + P)
                    nc.tensor.matmul(dst[:, :], ht_hi[i][:, row], w2[:, m, :], start=(m == 0), stop=False)
                    last = nc.tensor.matmul(dst[:, :], ht_lo[i][:, row], w2[:, m, :], start=False, stop=(m == M - 1))
                    if p == 3 and m == M - 1:
                        last.then_inc(down_done, 1)
                    if sums:
                        square_sum(m % 4).then_inc(hss_done, 1)

            def square_sum(n):
                i, u = n // 2, n % 2
                return nc.tensor.matmul(up_ps[:, i:i + 1], hh_sum[:, u * R + i * P:u * R + (i + 1) * P], ones_col[:, :],
                                        start=(u == 0), stop=(u == 1))

            def ternary(n):
                pe.wait_ge(abs_ready, n + 1)
                need(pe, tscale_ready, n)
                need(pe, relu_ready, piece(n // TERN, 0))
                nc.tensor.matmul(up_ps[:, :], group_ones[:, :], abs_w[n % TABS], start=True, stop=True).then_inc(gsum_done, 1)

            def normed_rows(t, dst):
                pe.wait_ge(x1n_ready, t + 1)
                transpose4(dst, x1n, ft_done)

            def values_of(t, b):
                pe.wait_ge(plo_ready, 4 * t + b + 1)
                for u in range(4):
                    h = slice((4 * u + b) * HD, (4 * u + b + 1) * HD)
                    q = slice(u * P, (u + 1) * P)
                    nc.tensor.matmul(mix_ps[:, h], pt_hi[b % 2][:, q], v_hi[:, h], start=True, stop=False)
                    nc.tensor.matmul(mix_ps[:, h], pt_hi[b % 2][:, q], v_lo[:, h], start=False, stop=False)
                    last = nc.tensor.matmul(mix_ps[:, h], pt_lo[b % 2][:, q], v_hi[:, h], start=False, stop=True)
                last.then_inc(pv_done, 1)

            def probs_t(t, b):
                pe.wait_ge(exp_ready, 4 * t + b + 1)
                transpose4((tr_a, tr_b)[b % 2], p_sb[b], pt_done)

            def project_out(t):
                if isinstance(t, int) and t == 0:
                    pe.wait_ge(w_lo_ready[3], 1)
                pe.wait_ge(alo_ready, t + 1)
                project(o_ps, at_hi, at_lo, 3, o_done)

            def slot(g, j, tern, up, down):
                t = J * g + j
                more, first = not last_slot(t), isinstance(t, int) and t == 0
                pe.wait_ge(qn_ready, t + 1)
                if first:
                    pe.wait_ge(xlo_ready, 1)
                else:
                    pe.wait_ge(alo_ready, t)
                transpose4(tr_a, qn, qt_done)
                if not first:
                    project_out(t - 1)
                pe.wait_ge(kn_ready, t + 1)
                if more:
                    pe.wait_ge(ctx_top_ready, t + 2)
                transpose4(tr_b, kn, kt_done)
                if down:
                    ffn_down(g, j, 0, mix_ps)
                if tern and t == 2:
                    pe.wait_ge(fc_top_part, 1)
                    spread(up_ps, fc_top[:, :], fc_top_spread)
                    pe.wait_ge(ffn_consts, 1)
                for n in units(t, 0, tern):
                    ternary(n)
                if more:
                    pe.wait_ge(xn_ready, t + 2)
                    pe.wait_ge(qlo_ready, t + 1)
                    transpose4(tr_a, xn, xt_done)
                pe.wait_ge(qlo_ready, t + 1)
                pe.wait_ge(klo_ready, t + 1)
                pe.wait_ge(qraw_ready, t + 1)
                pe.wait_ge(kraw_ready, t + 1)
                pe.wait_ge(vlo_ready, t + 1)
                need(pe, x1_ready, t)
                for u in range(4):
                    col = slice(u * P, (u + 1) * P)
                    for n, (q, k) in enumerate(((qt_hi, kt_hi), (qt_hi, kt_lo), (qt_lo, kt_hi))):
                        for b in range(4):
                            row = slice(b * HD, (b + 1) * HD)
                            last = nc.tensor.matmul(score_ps[b][:, col], q[row, col], k[row, col], start=(n == 0),
                                                    stop=(n == 2))
                last.then_inc(s_done, 1)
                if not first:
                    normed_rows(t - 1, tr_b)
                for p in range(1, 4):
                    if down:
                        ffn_down(g, j, p, mix_ps)
                    for n in units(t, p, tern):
                        ternary(n)
                if more:
                    pe.wait_ge(xlo_ready, t + 2)
                probs_t(t, 0)
                for n in units(t, 4, tern):
                    ternary(n)
                if up:
                    if tern:
                        pe.wait_ge(tscale_ready, TERN * t + TERN)
                        pe.wait_ge(tern_ready, NU)
                    ffn_up(g, j, 0, up_ps)
                need(pe, flo_ready, t)
                probs_t(t, 1)
                if more:
                    project(q_ps, xt_hi, xt_lo, 0, q_done)
                if down:
                    pe.wait_ge(out_ready, t - LAG + 1)
                elif first:
                    pe.wait_ge(setup_dve, 1)
                else:
                    pe.wait_ge(attn_ready, t)
                values_of(t, 0)
                probs_t(t, 2)
                values_of(t, 1)
                for n in units(t, 5, tern):
                    ternary(n)
                if up:
                    ffn_up(g, j, 1, up_ps)
                probs_t(t, 3)
                values_of(t, 2)
                if more:
                    pe.wait_ge(clo_ready, t + 2)
                    project(k_ps, ct_hi, ct_lo, 1, k_done)
                values_of(t, 3)
                for n in units(t, 6, tern):
                    ternary(n)
                if up:
                    ffn_up(g, j, 2, up_ps)
                if not (isinstance(t, int) and t + 2 >= NT):
                    pe.wait_ge(ctx_part_ready, t + 3)
                    spread(tr_b, ctx_part[:, :], ctx_spread)
                pe.wait_ge(attn_ready, t + 1)
                transpose4(tr_a, attn, at_done)
                if more:
                    project(v_ps, ct_hi, ct_lo, 2, v_done)
                for n in units(t, 7, tern):
                    ternary(n)
                if up:
                    ffn_up(g, j, 3, up_ps)

            def spread_weight(s):
                pe.wait_ge(w_top_part, s + 1)
                if s == 0:
                    pe.wait_ge(ctx_top_ready, 1)
                else:
                    pe.wait_ge(w_top_ready, s)
                spread(tr_b, w_top[:, s:s + 1], w_top_spread)

            pe.wait_ge(consts_ready, 5)
            pe.wait_ge(ctx_part_ready, 1)
            spread(tr_b, ctx_part[:, :], ctx_spread)
            pe.wait_ge(xn_ready, 1)
            transpose4(tr_a, xn, xt_done)
            spread_weight(0)
            spread_weight(1)
            pe.wait_ge(w_lo_ready[0], 1)
            pe.wait_ge(xlo_ready, 1)
            project(q_ps, xt_hi, xt_lo, 0, q_done)
            spread_weight(2)
            pe.wait_ge(w_lo_ready[1], 1)
            pe.wait_ge(clo_ready, 1)
            project(k_ps, ct_hi, ct_lo, 1, k_done)
            spread_weight(3)
            pe.wait_ge(w_lo_ready[2], 1)
            project(v_ps, ct_hi, ct_lo, 2, v_done)
            pe.wait_ge(vb_ready, 1)
            pe.wait_ge(stage_in[3], 16)
            for c in range(C):
                last = nc.tensor.matmul(mix_ps[:, :], vb_wide[:, c, :], stage[3][:, c * D:(c + 1) * D], start=(c == 0),
                                        stop=(c == C - 1))
            last.then_inc(wov_done, 1)
            pe.wait_ge(ctx_part_ready, 2)
            pe.wait_ge(w_top_ready, 4)
            spread(tr_b, ctx_part[:, :], ctx_spread)
            for j in range(J):
                slot(0, j, True, j >= 2, False)
            pe.wait_ge(tern_ready, 2 * NU)
            with pe.Fori(1, NG - 1) as g:
                for j in range(J):
                    slot(g, j, False, True, True)
            for j in range(J):
                slot(NG - 1, j, False, True, True)
            project_out(NT - 1)
            for p in range(4):
                ffn_down(NG, 0, p, mix_ps)
            pe.wait_ge(klo_ready, NT)
            normed_rows(NT - 1, tr_b)
            for p in range(4):
                ffn_down(NG, 1, p, tr_a)
            for j in range(2):
                for f in range(UP):
                    ffn_up(NG, j, f, score_ps[f], 4)
            pe.wait_ge(out_ready, NT - 3)
            for p in range(4):
                ffn_down(NG, 2, p, mix_ps, 4)
            pe.wait_ge(out_ready, NT - 2)
            for p in range(4):
                ffn_down(NG, 3, p, tr_a)

        @block.scalar
        def _(act):
            def copy_hi(dst, src, done, scale=1.0):
                nc.scalar.activation(dst, src, ACT.Copy, scale=scale).then_inc(done, 1)

            def x_hi(t):
                act.wait_ge(xt_done, t + 1)
                need(act, q_done, t)
                copy_hi(xt_hi[:, :], tr_a[:, :], xhi_ready)

            def context_hi(t, par):
                act.wait_ge(ctx_scale_ready, t + 1)
                need(act, v_done, t)
                nc.scalar.activation(ct_hi[:, :], ctx_sb[par][:, :], ACT.Identity,
                                     scale=ctx_scale[:, :]).then_inc(chi_ready, 1)

            def square_sum(t, raw, raw_ready, n, total, done):
                act.wait_ge(raw_ready, t + 1)
                need(act, done, t)
                nc.scalar.activation(square_out[n][:, :], raw[:, :], ACT.Square,
                                     accum_out=total[:, :]).then_inc(done, 1)

            def v_hi_of(t):
                act.wait_ge(v_done, t + 1)
                need(act, pv_done, 4 * t)
                copy_hi(v_hi[:, :], v_ps[:, :], vhi_ready, V_SCALE)

            def relu_hi(g, j, f, src):
                t = J * g + j
                k = piece(t, f)
                n = UP * (j % 2) + f
                act.wait_ge(up_done, k + 1)
                need(act, h_ready, k - 1)
                need(act, hhi_ready, k - 1)
                nc.scalar.activation(relu_sb[f % 2][:, :], src[:, :], ACT.Relu, scale=relu_scale[:, :]).then_inc(relu_ready, 1)
                act.wait_ge(relu_ready, k + 1)
                nc.scalar.activation(ht_hi[(j // 2 + 1) % 2][:, n * 512:(n + 1) * 512], relu_sb[f % 2][:, :],
                                     ACT.Square).then_inc(hhi_ready, 1)

            def squares(g, j, f):
                k, n = piece(J * g + j, f), UP * (j % 2) + f
                act.wait_ge(h_ready, k + 1)
                if n == 0:
                    need(act, hss_done, 4 * pairs_before(g, j))
                    dst = hh_sum
                else:
                    need(act, hsum_ready, (2 * UP - 1) * pairs_before(g, j) + max(0, n - 2))
                    dst = hh_sb[f % 2]
                nc.scalar.activation(dst[:, :], h_sb[f % 2][:, :], ACT.Square).then_inc(hh_ready, 1)

            def ternary(n):
                if n >= 2 * NU:
                    return
                s, loads = ternary_stage(n // 4)
                if n % 4 == 0:
                    act.wait_ge(stage_in[s], 16 * loads)
                src = stage[s][:, (n % 4) * 512:(n % 4 + 1) * 512]
                need(act, gsum_done, n - TABS + 1)
                need(act, tmask_ready, n - TABS + 1)
                nc.scalar.activation(abs_w[n % TABS], src, ACT.Abs, scale=2.0).then_inc(abs_ready, 1)
                nc.scalar.activation(ternary_place(n), src, ACT.Sign).then_inc(sign_ready, 1)

            def normed_hi(t, j):
                act.wait_ge(ft_done, t + 1)
                nc.scalar.activation(ft_hi[j // 2][:, :, j % 2 * P:(j % 2 + 1) * P],
                                     tr_b[:, :].rearrange("p (c t) -> p c t", c=C), ACT.Copy).then_inc(fhi_ready, 1)

            def exps(t, b):
                act.wait_ge(bias_ready, 4 * t + b + 1)
                need(act, pt_done, 4 * t + b - 3)
                if b == 0:
                    need(act, pinv_ready, t)
                for u in range(4):
                    h = 4 * u + b
                    last = nc.scalar.activation(p_sb[b][:, u * P:(u + 1) * P], score_ps[b][:, u * P:(u + 1) * P],
                                                ACT.Exp, scale=exp_scale[:, :], bias=exp_bias[:, h:h + 1],
                                                accum_out=p_sum[:, h:h + 1])
                last.then_inc(exp_ready, 1)

            def probs_hi(t, b):
                act.wait_ge(pt_done, 4 * t + b + 1)
                need(act, pv_done, 4 * t + b - 1)
                copy_hi(pt_hi[b % 2][:, :], (tr_a, tr_b)[b % 2][:, :], phi_ready)

            def slot(g, j, tern, up, down):
                t = J * g + j
                more, first = not last_slot(t), isinstance(t, int) and t == 0
                started = isinstance(t, int) and t == 2
                act.wait_ge(qt_done, t + 1)
                need(act, s_done, t)
                copy_hi(qt_hi[:, :], tr_a[:, :], qhi_ready)
                if up and not started:
                    squares(g, j - 1, 3)
                act.wait_ge(kt_done, t + 1)
                copy_hi(kt_hi[:, :], tr_b[:, :], khi_ready)
                if more:
                    context_hi(t + 1, (j + 1) % 2)
                for n in units(t, 0, tern):
                    ternary(n + TAHEAD)
                if more:
                    x_hi(t + 1)
                exps(t, 0)
                for n in units(t, 1, tern):
                    ternary(n + TAHEAD)
                exps(t, 1)
                if not first:
                    normed_hi(t - 1, (j - 1) % J)
                for n in units(t, 2, tern):
                    ternary(n + TAHEAD)
                exps(t, 2)
                probs_hi(t, 0)
                exps(t, 3)
                for n in units(t, 3, tern):
                    ternary(n + TAHEAD)
                probs_hi(t, 1)
                if up:
                    relu_hi(g, j, 0, up_ps)
                    squares(g, j, 0)
                for n in units(t, 4, tern):
                    ternary(n + TAHEAD)
                probs_hi(t, 2)
                if more:
                    square_sum(t + 1, q_raw, qraw_ready, 0, q_ss, qss_ready)
                if up:
                    relu_hi(g, j, 1, up_ps)
                probs_hi(t, 3)
                if up:
                    squares(g, j, 1)
                for n in units(t, 5, tern):
                    ternary(n + TAHEAD)
                if more:
                    square_sum(t + 1, k_raw, kraw_ready, 1, k_ss, kss_ready)
                if up:
                    relu_hi(g, j, 2, up_ps)
                for n in units(t, 6, tern):
                    ternary(n + TAHEAD)
                act.wait_ge(at_done, t + 1)
                need(act, o_done, t)
                copy_hi(at_hi[:, :], tr_a[:, :], ahi_ready)
                if up:
                    squares(g, j, 2)
                if more:
                    v_hi_of(t + 1)
                if up:
                    relu_hi(g, j, 3, up_ps)
                for n in units(t, 7, tern):
                    ternary(n + TAHEAD)

            for s in range(4):
                act.wait_ge(w_scale_ready, s + 1)
                nc.scalar.activation(w_hi[s][:, :, :].rearrange("p c n -> p (c n)"), stage[s], ACT.Identity,
                                     scale=w_scale[:, s:s + 1]).then_inc(w_hi_ready, 1)
                if s == 0:
                    x_hi(0)
                    act.wait_ge(small_in, 16 * 7)
                    nc.scalar.activation(gain[:, :], gain_in[:, :], ACT.Tanh).then_inc(gain_ready, 1)
                if s == 1:
                    context_hi(0, 0)
                    square_sum(0, q_raw, qraw_ready, 0, q_ss, qss_ready)
                if s == 2:
                    square_sum(0, k_raw, kraw_ready, 1, k_ss, kss_ready)
            v_hi_of(0)
            for n in range(TAHEAD):
                ternary(n)
            for j in range(J):
                slot(0, j, True, j >= 2, False)
            with act.Fori(1, NG - 1) as g:
                for j in range(J):
                    slot(g, j, False, True, True)
            for j in range(J):
                slot(NG - 1, j, False, True, True)
            squares(NG - 1, J - 1, 3)
            normed_hi(NT - 1, J - 1)
            for j in range(2):
                for f in range(UP):
                    relu_hi(NG, j, f, score_ps[f])
                    if j or f:
                        squares(NG, j - (f == 0), (f - 1) % UP)
            squares(NG, 1, UP - 1)

        @block.vector
        def _(dve):
            def sub_lo(dst, src, hi, hi_ready, n, done):
                dve.wait_ge(hi_ready, n)
                nc.vector.tensor_tensor(dst, src, hi, ALU.subtract).then_inc(done, 1)

            def row_stats(src, raw, mv, pair, done, n):
                first = held(dve, 4 * n + 1)
                nc.vector.bn_stats(raw[:, :], src).then_inc(done, 1)
                dve.wait_ge(consts_ready, 5)
                dve.wait_ge(done, first)
                nc.vector.bn_aggr(mv[:, :], raw[:, :]).then_inc(done, 1)
                dve.wait_ge(done, 4 * n + 2)
                nc.vector.tensor_scalar(pair[:, 0:1], mv[:, 0:1], -1.0, None, ALU.mult).then_inc(done, 1)
                nc.vector.tensor_scalar(pair[:, 1:2], mv[:, 1:2], LN_EPS, X_SCALE ** -2, ALU.add,
                                        ALU.mult).then_inc(done, 1)

            def x_stats(t, b, times):
                dve.wait_ge(x_in[b], 16 * times)
                need(dve, xn_ready, t)
                row_stats(x_sb[b][:, :], ln1_raw, ln1_mv, ln1_in, ln1_ready, t)

            def context_max(t, par, times):
                dve.wait_ge(ctx_in[par], 16 * times)
                need(dve, ctx_spread, t)
                nc.vector.tensor_reduce(ctx_part[:, :], ctx_sb[par][:, :], AX.X, ALU.max,
                                        apply_absolute_value=True).then_inc(ctx_part_ready, 1)

            def context_top(t):
                dve.wait_ge(ctx_spread, t + 1)
                need(dve, ctx_step_ready, 3 * t)
                nc.vector.tensor_reduce(ctx_top[:, :], tr_b[:, 0:P], AX.X, ALU.max).then_inc(ctx_top_ready, 1)

            def output_scale(par):
                nc.vector.tensor_scalar(o_unscale[par][:, :], ctx_top[:, :], TINY, o_unscale0[:, :], ALU.max,
                                        ALU.mult).then_inc(ctx_step_ready, 1)

            def context_scale(t, par):
                dve.wait_ge(ctx_top_ready, t + 1)
                need(dve, chi_ready, t)
                need(dve, clo_ready, t)
                need(dve, kraw_ready, t)
                need(dve, x1_ready, t - 1)
                nc.vector.tensor_scalar(ctx_step[:, :], ctx_top[:, :], TINY, 1.0 / C_MAX, ALU.max,
                                        ALU.mult).then_inc(ctx_step_ready, 1)
                nc.vector.tensor_scalar(k_unscale[:, :], ctx_top[:, :], TINY, k_unscale0[:, :], ALU.max,
                                        ALU.mult).then_inc(ctx_step_ready, 1)
                if not isinstance(t, int) or t > 0:
                    output_scale(par)
                dve.wait_ge(ctx_step_ready, 3 * t + (2 if isinstance(t, int) and t == 0 else 3))
                nc.vector.reciprocal(ctx_scale[:, :], ctx_step[:, :]).then_inc(ctx_scale_ready, 1)

            def x_lo(t):
                need(dve, q_done, t)
                sub_lo(xt_lo[:, :], tr_a[:, :], xt_hi[:, :], xhi_ready, t + 1, xlo_ready)

            def context_lo(t, par):
                dve.wait_ge(chi_ready, t + 1)
                dve.wait_ge(ctx_scale_ready, t + 1)
                need(dve, v_done, t)
                nc.vector.scalar_tensor_tensor(out=ct_lo[:, :], in0=ctx_sb[par][:, :], scalar=ctx_scale[:, :],
                                               in1=ct_hi[:, :], op0=ALU.mult, op1=ALU.subtract).then_inc(clo_ready, 1)

            def q_out(t):
                dve.wait_ge(q_done, t + 1)
                need(dve, qn_ready, t)
                nc.vector.scalar_tensor_tensor(out=q_raw[:, :], in0=q_ps[:, :], scalar=q_unscale[:, :], in1=qb_sb[:, :],
                                               op0=ALU.mult, op1=ALU.add).then_inc(qraw_ready, 1)

            def k_out(t):
                dve.wait_ge(k_done, t + 1)
                need(dve, kn_ready, t)
                nc.vector.scalar_tensor_tensor(out=k_raw[:, :], in0=k_ps[:, :], scalar=k_unscale[:, :], in1=kb_sb[:, :],
                                               op0=ALU.mult, op1=ALU.add).then_inc(kraw_ready, 1)

            def k_norm(t):
                dve.wait_ge(krms_ready, t + 1)
                need(dve, kt_done, t)
                nc.vector.scalar_tensor_tensor(out=kn[:, :], in0=k_raw[:, :], scalar=k_rms[:, :], in1=qk_norm[:, :],
                                               op0=ALU.mult, op1=ALU.mult).then_inc(kn_ready, 1)

            def v_lo_of(t):
                dve.wait_ge(vhi_ready, t + 1)
                need(dve, pv_done, 4 * t)
                nc.vector.scalar_tensor_tensor(out=v_lo[:, :], in0=v_ps[:, :], scalar=V_SCALE, in1=v_hi[:, :],
                                               op0=ALU.mult, op1=ALU.subtract).then_inc(vlo_ready, 1)

            def hidden(g, j, f):
                k = piece(J * g + j, f)
                dve.wait_ge(relu_ready, k + 1)
                need(dve, hh_ready, k - 1)
                need(dve, hlo_ready, k - 1)
                nc.vector.tensor_tensor(h_sb[f % 2][:, :], relu_sb[f % 2][:, :], relu_sb[f % 2][:, :],
                                        ALU.mult).then_inc(h_ready, 1)

            def hidden_lo(g, j, f):
                k = piece(J * g + j, f)
                n = UP * (j % 2) + f
                i = (j // 2 + 1) % 2
                dve.wait_ge(h_ready, k + 1)
                sub_lo(ht_lo[i][:, n * 512:(n + 1) * 512], h_sb[f % 2][:, :], ht_hi[i][:, n * 512:(n + 1) * 512], hhi_ready,
                       k + 1, hlo_ready)

            def ffn_out(g, j, src):
                dve.wait_ge(down_done, J * g + j - LAG + 1)
                dve.wait_ge(hgain_ready, pairs_before(g, j))
                dve.wait_ge(out_free[j % 2], 16 * (2 * g - 1 + j // 2))
                nc.vector.scalar_tensor_tensor(out=out_sb[j % 2][:, :], in0=src[:, :], scalar=h_gain[:, j % 2:j % 2 + 1],
                                               in1=x1[j][:, :], op0=ALU.mult, op1=ALU.add).then_inc(out_ready, 1)

            def hidden_mean_square(g, j):
                n = pairs_before(g, j)
                dve.wait_ge(hss_done, 4 * n)
                nc.vector.tensor_scalar(h_ms[:, :], up_ps[:, 0:2], ms_scale[:, :], FFN_EPS, ALU.mult,
                                        ALU.add).then_inc(hms_ready, 1)

            def ternary(n):
                dve.wait_ge(gsum_done, n + 1)
                need(dve, tsigned_ready, n - TD + 1)
                nc.vector.tensor_scalar(t_scale[n % TD], up_ps[:, :], 0.5 / GROUP, TERNARY_CLIP, ALU.mult,
                                        ALU.max).then_inc(tscale_ready, 1)
                dve.wait_ge(tscale_ready, n + 1)
                need(dve, tern_ready, n - TD + 1)
                nc.vector.tensor_tensor(t_mask[n % TD], abs_w[n % TABS], t_scale[n % TD], ALU.is_gt).then_inc(tmask_ready, 1)
                if n < NU:
                    need(dve, tmax_ready, n)
                    nc.vector.tensor_tensor(scale_top[:, :], scale_top[:, :], t_scale[n % TD], ALU.max).then_inc(tmax_ready, 1)

            def normed_lo(t, j):
                dve.wait_ge(fhi_ready, t + 1)
                col = slice(j % 2 * P, (j % 2 + 1) * P)
                nc.vector.tensor_tensor(ft_lo[j // 2][:, :, col], tr_b[:, :].rearrange("p (c t) -> p c t", c=C),
                                        ft_hi[j // 2][:, :, col], ALU.subtract).then_inc(flo_ready, 1)

            def score_top(t, b):
                if b == 0:
                    dve.wait_ge(s_done, t + 1)
                    need(dve, exp_ready, 4 * t)
                nc.vector.tensor_reduce(s_top[:, b:H:4], score_ps[b][:, :].rearrange("p (u k) -> p u k", k=P), AX.X,
                                        ALU.max).then_inc(top_ready, 1)
                dve.wait_ge(top_ready, 4 * t + b + 1)
                nc.vector.tensor_scalar(exp_bias[:, b:H:4], s_top[:, b:H:4], neg_exp_scale[:, :], LOG_P_SCALE, ALU.mult,
                                        ALU.add).then_inc(bias_ready, 1)

            def probs_lo(t, b):
                need(dve, pv_done, 4 * t + b - 1)
                sub_lo(pt_lo[b % 2][:, :], (tr_a, tr_b)[b % 2][:, :], pt_hi[b % 2][:, :], phi_ready, 4 * t + b + 1, plo_ready)

            def x1_out(t, j):
                dve.wait_ge(o_done, t + 1)
                dve.wait_ge(xb_ready, t + 1)
                nc.vector.scalar_tensor_tensor(out=x1[j][:, :], in0=o_ps[:, :], scalar=o_unscale[j % 2][:, :], in1=xb[:, :],
                                               op0=ALU.mult, op1=ALU.add).then_inc(x1_ready, 1)

            def x1_stats(t, j):
                dve.wait_ge(x1_ready, t + 1)
                need(dve, x1n_ready, t)
                row_stats(x1[j][:, :], ln2_raw, ln2_mv, ln2_in, ln2_ready, t)

            def attention(t):
                dve.wait_ge(pv_done, 4 * t + 4)
                dve.wait_ge(pinv_ready, t + 1)
                need(dve, at_done, t)
                nc.vector.tensor_tensor(attn[:, :].rearrange("p (h d) -> p h d", d=HD),
                                        mix_ps[:, :].rearrange("p (h d) -> p h d", d=HD),
                                        p_inv[:, :].unsqueeze(2).to_broadcast([P, H, HD]), ALU.mult).then_inc(attn_ready, 1)

            step = [0]

            def chain(ins):
                step[0] += 1
                ins.then_inc(dve_step, 1)
                dve.wait_ge(dve_step, step[0])

            def ffn_scales():
                dve.wait_ge(fc_top_spread, 1)
                chain(nc.vector.tensor_reduce(fc_top_all[:, :], up_ps[:, 0:P], AX.X, ALU.max))
                chain(nc.vector.tensor_scalar(tmp_c[:, 1:2], fc_top_all[:, :], D * X_SCALE / R_MAX, None, ALU.mult))
                chain(nc.vector.reciprocal(relu_scale[:, :], tmp_c[:, 1:2]))
                chain(nc.vector.tensor_scalar(tmp_c[:, 1:2], fc_top_all[:, :], D / R_MAX, None, ALU.mult))
                chain(nc.vector.tensor_tensor(h_unscale[:, :], tmp_c[:, 1:2], tmp_c[:, 1:2], ALU.mult))
                chain(nc.vector.tensor_tensor(tmp_c[:, 0:1], h_unscale[:, :], h_unscale[:, :], ALU.mult))
                chain(nc.vector.tensor_scalar(ms_scale[:, :], tmp_c[:, 0:1], 1.0 / HID, None, ALU.mult))
                nc.vector.tensor_tensor(out_gain[:, :], h_unscale[:, :], gain[:, 1:2], ALU.mult).then_inc(ffn_consts, 1)

            def slot(g, j, tern, up, down):
                t = J * g + j
                more, first = not last_slot(t), isinstance(t, int) and t == 0
                started = isinstance(t, int) and t == 2
                two_more = not (isinstance(t, int) and t + 2 >= NT)
                need(dve, s_done, t)
                sub_lo(qt_lo[:, :], tr_a[:, :], qt_hi[:, :], qhi_ready, t + 1, qlo_ready)
                if up and not started:
                    hidden_lo(g, j - 1, 3)
                if not first:
                    x1_out(t - 1, (j - 1) % J)
                sub_lo(kt_lo[:, :], tr_b[:, :], kt_hi[:, :], khi_ready, t + 1, klo_ready)
                if more:
                    context_scale(t + 1, (j + 1) % 2)
                if started:
                    ffn_scales()
                if not first:
                    x1_stats(t - 1, (j - 1) % J)
                for n in units(t, 0, tern):
                    ternary(n)
                if more:
                    context_lo(t + 1, (j + 1) % 2)
                    x_lo(t + 1)
                for b in range(4):
                    score_top(t, b)
                for p in range(1, 4):
                    for n in units(t, p, tern):
                        ternary(n)
                if down and j % 2 == 0:
                    hidden_mean_square(g, j)
                if two_more:
                    x_stats(t + 2, (j + 2) % 4, g + 1 + (j + 2) // J)
                    context_max(t + 2, j % 2, 2 * g + 1 + (j + 2) // 2)
                if not first:
                    normed_lo(t - 1, (j - 1) % J)
                if down:
                    ffn_out(g, j, mix_ps)
                probs_lo(t, 0)
                for n in units(t, 4, tern):
                    ternary(n)
                probs_lo(t, 1)
                if up:
                    hidden(g, j, 0)
                    hidden_lo(g, j, 0)
                if more:
                    q_out(t + 1)
                probs_lo(t, 2)
                for n in units(t, 5, tern):
                    ternary(n)
                if up:
                    hidden(g, j, 1)
                probs_lo(t, 3)
                if up:
                    hidden_lo(g, j, 1)
                dve.wait_ge(exp_ready, 4 * t + 4)
                need(dve, attn_ready, t)
                nc.vector.reciprocal(p_inv[:, :], p_sum[:, :]).then_inc(pinv_ready, 1)
                if more:
                    k_out(t + 1)
                attention(t)
                if more:
                    k_norm(t + 1)
                for n in units(t, 6, tern):
                    ternary(n)
                if up:
                    hidden(g, j, 2)
                    hidden_lo(g, j, 2)
                if two_more:
                    context_top(t + 2)
                need(dve, o_done, t)
                sub_lo(at_lo[:, :], tr_a[:, :], at_hi[:, :], ahi_ready, t + 1, alo_ready)
                if more:
                    v_lo_of(t + 1)
                for n in units(t, 7, tern):
                    ternary(n)
                if up:
                    hidden(g, j, 3)
                if isinstance(t, int) and t == 1:
                    dve.wait_ge(tmax_ready, NU)
                    nc.vector.tensor_reduce(fc_top[:, :], scale_top[:, :], AX.X, ALU.max).then_inc(fc_top_part, 1)

            def weight_max(s):
                dve.wait_ge(stage_in[s], 16)
                nc.vector.tensor_reduce(w_top[:, s:s + 1], stage[s], AX.X, ALU.max,
                                        apply_absolute_value=True).then_inc(w_top_part, 1)

            def weight_scale(s):
                dve.wait_ge(w_top_spread, s + 1)
                nc.vector.tensor_reduce(w_top_all[:, s:s + 1], tr_b[:, 0:P], AX.X, ALU.max).then_inc(w_top_ready, 1)
                dve.wait_ge(w_top_ready, s + 1)
                nc.vector.tensor_scalar(w_step[:, s:s + 1], w_top_all[:, s:s + 1], TINY, 1.0 / W_MAX, ALU.max,
                                        ALU.mult).then_inc(w_step_ready, 1)
                dve.wait_ge(w_step_ready, s + 1)
                nc.vector.reciprocal(w_scale[:, s:s + 1], w_step[:, s:s + 1]).then_inc(w_scale_ready, 1)

            def weight_lo(s):
                dve.wait_ge(w_scale_ready, s + 1)
                dve.wait_ge(w_hi_ready, s + 1)
                nc.vector.scalar_tensor_tensor(out=w_lo[s][:, :, :].rearrange("p c n -> p (c n)"), in0=stage[s],
                                               scalar=w_scale[:, s:s + 1],
                                               in1=w_hi[s][:, :, :].rearrange("p c n -> p (c n)"), op0=ALU.mult,
                                               op1=ALU.subtract).then_inc(w_lo_ready[s], 1)

            nc.vector.memset(ones_col[:, :], 1.0).then_inc(consts_ready, 1)
            nc.vector.memset(minus_half[:, :], -0.5).then_inc(consts_ready, 1)
            chain(nc.vector.memset(scale_top[:, :], 0.0))
            chain(nc.vector.memset(group_ones[:, :], 0.0))
            for r in range(0, P, GROUP):
                nc.vector.memset(group_ones[r:r + GROUP, r:r + GROUP], 1.0).then_inc(consts_ready, 1)
            for i in range(2):
                nc.vector.memset(tmp_c[:, i:i + 1], 0.0).then_inc(out_free[i], 16)
            dve.wait_ge(consts_ready, 5)
            x_stats(0, 0, 1)
            context_max(0, 0, 1)
            context_top(0)
            weight_max(0)
            weight_scale(0)
            weight_max(1)
            x_lo(0)
            weight_scale(1)
            chain(nc.vector.tensor_scalar(k_unscale0[:, :], w_step[:, 1:2], 1.0 / C_MAX, None, ALU.mult))
            context_scale(0, 0)
            chain(nc.vector.tensor_scalar(q_unscale[:, :], w_step[:, 0:1], 1.0 / X_SCALE, None, ALU.mult))
            weight_lo(0)
            weight_max(2)
            weight_lo(1)
            weight_scale(2)
            context_lo(0, 0)
            dve.wait_ge(small_in, 16 * 7)
            q_out(0)
            chain(nc.vector.tensor_tensor(qk_norm[:, :], qk_norm[:, :], nk_in[:, :], ALU.mult))
            chain(nc.vector.tensor_reduce(qk_top[:, :], qk_norm[:, :], AX.X, ALU.max, apply_absolute_value=True))
            chain(nc.vector.tensor_scalar(qk_top[:, :], qk_top[:, :], TINY, None, ALU.max))
            chain(nc.vector.reciprocal(qk_inv[:, :], qk_top[:, :]))
            chain(nc.vector.tensor_scalar(qk_norm[:, :], qk_norm[:, :], qk_inv[:, :], QK_SCALE, ALU.mult, ALU.mult))
            unit = float(HD) ** -0.5 / QK_SCALE ** 2
            chain(nc.vector.tensor_scalar(exp_scale[:, :], qk_top[:, :], unit, None, ALU.mult))
            chain(nc.vector.tensor_scalar(neg_exp_scale[:, :], qk_top[:, :], -unit, None, ALU.mult))
            k_out(0)
            weight_lo(2)
            k_norm(0)
            weight_max(3)
            weight_scale(3)
            x_stats(1, 1, 1)
            context_max(1, 1, 1)
            chain(nc.vector.tensor_copy(vb_wide, vb_col[:, :].unsqueeze(2).to_broadcast([P, C, P])))
            nc.vector.memset(tmp_c[:, 3:4], 0.0).then_inc(vb_ready, 1)
            dve.wait_ge(gain_ready, 1)
            chain(nc.vector.tensor_tensor(tmp_c[:, 0:1], w_step[:, 2:3], w_step[:, 3:4], ALU.mult))
            chain(nc.vector.tensor_scalar(o_unscale0[:, :], tmp_c[:, 0:1], gain[:, 0:1], 1.0 / (V_SCALE * C_MAX), ALU.mult,
                                          ALU.mult))
            output_scale(0)
            v_lo_of(0)
            weight_lo(3)
            context_top(1)
            dve.wait_ge(wov_done, 1)
            chain(nc.vector.tensor_tensor(o_const[:, :], mix_ps[:, :], ob_in[:, :], ALU.add))
            chain(nc.vector.tensor_scalar(o_const[:, :], o_const[:, :], gain[:, 0:1], None, ALU.mult))
            nc.vector.memset(tmp_c[:, 2:3], 0.0).then_inc(setup_dve, 1)
            for j in range(J):
                slot(0, j, True, j >= 2, False)
            dve.wait_ge(tern_ready, 2 * NU)
            with dve.Fori(1, NG - 1) as g:
                for j in range(J):
                    slot(g, j, False, True, True)
            for j in range(J):
                slot(NG - 1, j, False, True, True)
            hidden_lo(NG - 1, J - 1, 3)
            x1_out(NT - 1, J - 1)
            x1_stats(NT - 1, J - 1)
            hidden_mean_square(NG, 0)
            ffn_out(NG, 0, mix_ps)
            normed_lo(NT - 1, J - 1)
            ffn_out(NG, 1, tr_a)
            for j in range(2):
                for f in range(UP):
                    hidden(NG, j, f)
                    hidden_lo(NG, j, f)
            hidden_mean_square(NG, 2)
            ffn_out(NG, 2, mix_ps)
            ffn_out(NG, 3, tr_a)

        @block.gpsimd
        def _(pool):
            def norm_rows(t, src, pair, pair_ready, rstd, rstd_ready, dst, done):
                count = held(pool, t + 1)
                if isinstance(t, int) and t == 0:
                    pool.wait_ge(consts_ready, 5)
                pool.wait_ge(pair_ready, 4 * t + 4)
                need(pool, done, t)
                nc.gpsimd.tensor_tensor(rstd[:, :], pair[:, 1:2], minus_half[:, 0:1], ALU.pow).then_inc(rstd_ready, 1)
                pool.wait_ge(consts_ready, 5)
                pool.wait_ge(rstd_ready, count)
                nc.gpsimd.tensor_scalar(dst, src, pair[:, 0:1], rstd[:, :], ALU.add, ALU.mult).then_inc(done, 1)

            def rms(t, ss, ss_ready, ms, ms_ready, scale, out_rms, done, used):
                count, before = held(pool, t + 1), held(pool, t)
                pool.wait_ge(consts_ready, 5)
                pool.wait_ge(ss_ready, count)
                need(pool, used, before)
                nc.gpsimd.tensor_scalar(ms[:, :], ss[:, :], scale ** -2 / D, QK_EPS * scale ** -2, ALU.mult,
                                        ALU.add).then_inc(ms_ready, 1)
                pool.wait_ge(ms_ready, count)
                nc.gpsimd.tensor_tensor(out_rms[:, :], ms[:, :], minus_half[:, 0:1], ALU.pow).then_inc(done, 1)

            def x_norm(t, b):
                need(pool, xt_done, t)
                norm_rows(t, x_sb[b][:, :], ln1_in, ln1_ready, ln1_rstd, ln1_rstd_ready, xn[:, :], xn_ready)

            def q_norm(t):
                rms(t, q_ss, qss_ready, q_ms, qms_ready, QK_SCALE, q_rms, qrms_ready, qn_ready)
                count, before = held(pool, t + 1), held(pool, t)
                pool.wait_ge(consts_ready, 5)
                pool.wait_ge(qrms_ready, count)
                need(pool, qt_done, before)
                nc.gpsimd.tensor_scalar(qn[:, :], q_raw[:, :], q_rms[:, :], 1.0, ALU.mult, ALU.mult).then_inc(qn_ready, 1)

            def k_rms_of(t):
                rms(t, k_ss, kss_ready, k_ms, kms_ready, 1.0, k_rms, krms_ready, kn_ready)

            def hidden_sum(g, j, f):
                n = UP * (j % 2) + f
                if n == 0:
                    return
                pool.wait_ge(hh_ready, piece(J * g + j, f) + 1)
                need(pool, hsum_ready, (2 * UP - 1) * pairs_before(g, j) + n - 1)
                nc.gpsimd.tensor_tensor(hh_sum[:, :], hh_sum[:, :], hh_sb[f % 2][:, :], ALU.add).then_inc(hsum_ready, 1)

            def hidden_gain(g, j):
                n = held(pool, pairs_before(g, j))
                t = J * g + j
                pool.wait_ge(hms_ready, n)
                nc.gpsimd.tensor_tensor(h_rms[:, :], h_ms[:, :], minus_half[:, :], ALU.pow).then_inc(hrms_ready, 1)
                pool.wait_ge(consts_ready, 5)
                pool.wait_ge(hrms_ready, n)
                nc.gpsimd.tensor_scalar(h_gain[:, :], h_rms[:, :], out_gain[:, :], 1.0, ALU.mult,
                                        ALU.mult).then_inc(hgain_ready, 1)

            def ternary(n):
                pool.wait_ge(sign_ready, n + 1)
                pool.wait_ge(tscale_ready, n + 1)
                nc.gpsimd.tensor_tensor(ternary_place(n), ternary_place(n), t_scale[n % TD], ALU.mult).then_inc(tsigned_ready, 1)
                pool.wait_ge(tsigned_ready, n + 1)
                pool.wait_ge(tmask_ready, n + 1)
                nc.gpsimd.tensor_tensor(ternary_place(n), ternary_place(n), t_mask[n % TD], ALU.mult).then_inc(tern_ready, 1)

            def x1_norm(t, j):
                need(pool, ft_done, t)
                norm_rows(t, x1[j][:, :], ln2_in, ln2_ready, ln2_rstd, ln2_rstd_ready, x1n[:, :], x1n_ready)

            def slot(g, j, tern, up, down):
                t = J * g + j
                more, first = not last_slot(t), isinstance(t, int) and t == 0
                started = isinstance(t, int) and t == 2
                if up and not started:
                    hidden_sum(g, j - 1, 3)
                if not first:
                    x1_norm(t - 1, (j - 1) % J)
                if first:
                    pool.wait_ge(setup_dve, 1)
                else:
                    pool.wait_ge(x1_ready, t)
                nc.gpsimd.tensor_tensor(xb[:, :], x_sb[j][:, :], o_const[:, :], ALU.add).then_inc(xb_ready, 1)
                for n in units(t, 0, tern):
                    ternary(n)
                if down and j % 2 == 0:
                    hidden_gain(g, j)
                for p in range(1, 4):
                    for n in units(t, p, tern):
                        ternary(n)
                if not (isinstance(t, int) and t + 2 >= NT):
                    x_norm(t + 2, (j + 2) % 4)
                for p in range(4, 6):
                    for n in units(t, p, tern):
                        ternary(n)
                if up:
                    hidden_sum(g, j, 0)
                if more:
                    q_norm(t + 1)
                if up:
                    hidden_sum(g, j, 1)
                if more:
                    k_rms_of(t + 1)
                for n in units(t, 6, tern):
                    ternary(n)
                if up:
                    hidden_sum(g, j, 2)
                for n in units(t, 7, tern):
                    ternary(n)

            nc.gpsimd.memset(ident[:, :], 0.0).then_inc(zeros_ready, 1)
            pool.wait_ge(zeros_ready, 1)
            nc.gpsimd.affine_select(out=ident[:, :], in_=ident[:, :], compare_op=ALU.not_equal, fill=1.0, base=0,
                                    pattern=[[-1, P]], channel_multiplier=1).then_inc(consts_ready, 1)
            x_norm(0, 0)
            q_norm(0)
            k_rms_of(0)
            x_norm(1, 1)
            for j in range(J):
                slot(0, j, True, j >= 2, False)
            with pool.Fori(1, NG - 1) as g:
                for j in range(J):
                    slot(g, j, False, True, True)
            for j in range(J):
                slot(NG - 1, j, False, True, True)
            hidden_sum(NG - 1, J - 1, 3)
            x1_norm(NT - 1, J - 1)
            hidden_gain(NG, 0)
            for j in range(2):
                for f in range(UP):
                    hidden_sum(NG, j, f)
            hidden_gain(NG, 2)


def kernel(x, ctx_2048, g_xattn, g_ffn, L0_xattn_q_w, L0_xattn_q_b, L0_xattn_k_w, L0_xattn_k_b, L0_xattn_v_w,
           L0_xattn_v_b, L0_xattn_k_img_w, L0_xattn_k_img_b, L0_xattn_v_img_w, L0_xattn_v_img_b, L0_xattn_o_w,
           L0_xattn_o_b, L0_xattn_norm_q_w, L0_xattn_norm_k_w, L0_xattn_norm_k_img_w, L0_ffn_W_fc, L0_ffn_W_proj):
    import numpy as np
    import concourse.bacc as bacc
    from concourse.bass_utils import run_bass_kernel_spmd

    def chunks(w_t):
        return np.ascontiguousarray(w_t.reshape(-1, P, w_t.shape[1]).transpose(1, 0, 2))

    def rows(v):
        return np.ascontiguousarray(np.broadcast_to(np.asarray(v).reshape(1, -1), (P, np.asarray(v).size)))

    x = np.asarray(x)
    c = np.asarray(ctx_2048)
    nt, s, d = c.shape
    ctx_t = np.ascontiguousarray(c.reshape(nt, s, d // P, P).transpose(0, 3, 2, 1)).reshape(nt, P, d // P * s)
    flat = lambda w: chunks(np.asarray(w).T).reshape(P, -1)
    ins = {
        "x": np.ascontiguousarray(x), "ctx_t": ctx_t,
        "gains": rows(np.concatenate([np.asarray(g_xattn)[0:1], np.asarray(g_ffn)[0:1]])),
        "wq_t": flat(L0_xattn_q_w), "wk_t": flat(L0_xattn_k_img_w), "wv_t": flat(L0_xattn_v_img_w),
        "wo_t": flat(L0_xattn_o_w),
        "q_b": rows(L0_xattn_q_b), "k_b": rows(L0_xattn_k_img_b), "o_b": rows(L0_xattn_o_b),
        "norm_q": rows(L0_xattn_norm_q_w), "norm_k": rows(L0_xattn_norm_k_img_w),
        "v_b": np.ascontiguousarray(np.asarray(L0_xattn_v_img_b).reshape(d // P, P).T),
        "w_fc_t": chunks(np.asarray(L0_ffn_W_fc).T), "w_proj_t": chunks(np.asarray(L0_ffn_W_proj).T),
    }
    nc = bacc.Bacc("TRN2", target_bir_lowering=False, num_devices=1)
    args = {n: nc.dram_tensor(f"in_{n}", a.shape, mybir.dt.from_np(a.dtype), kind="ExternalInput").ap()
            for n, a in ins.items()}
    out = nc.dram_tensor("out", x.shape, F32, kind="ExternalOutput").ap()
    gated_cross_attention_kernel(nc, out=out, **args)
    got = run_bass_kernel_spmd(nc, [{f"in_{n}": a for n, a in ins.items()}], core_ids=[0])
    return got.results[0]["out"]
```

```python
from contextlib import ExitStack

import concourse.bass as bass
from concourse import mybir

F32 = mybir.dt.float32
F16 = mybir.dt.float16
BF16 = mybir.dt.bfloat16
ALU = mybir.AluOpType
ACT = mybir.ActivationFunctionType
AX = mybir.AxisListType

P = 128
LN_EPS = 1e-5
QK_EPS = 1e-6
FFN_EPS = 2.0 ** -23
TINY = 1e-30
GROUP = 64
TERNARY_CLIP = 1.001171767711639404296875e-08

X_SCALE = 2.0 ** 10
W_MAX = 2.0 ** 10
W_SUM = 2.0 ** 15
C_MAX = 2.0 ** 14
QK_SCALE = 2.0 ** 10
V_SCALE = 2.0 ** -18
LOG_P_SCALE = 9.70406052783923
R_MAX = 181.0


def gated_cross_attention_kernel(nc, x, ctx_t, gains, wq_t, wk_t, wv_t, wo_t, q_b, k_b, o_b, norm_q, norm_k, v_b,
                                 w_fc_t, w_proj_t, out):
    NT = x.shape[0]
    D = x.shape[2]
    C = D // P
    HID = w_fc_t.shape[2]
    M = HID // P
    HD = 32
    H = D // HD
    J = 4
    NG = NT // J
    R = 2 * P
    UP = 4
    LAG = 4
    NU = HID * D // (P * 512)
    TERN = 8
    PLACES = ((0, 2, 1, 1, 1, 1, 1, 1), (0, 1, 1, 1, 1, 1, 2, 1)) + ((1,) * 8,) * 2
    TD = 5
    TABS = 6
    TAHEAD = 4
    assert C == 4 and M == 4 * UP and H == 16 and NT % J == 0 and J * TERN == 2 * NU

    stack = ExitStack()
    with stack:
        def sb(name, shape, dt=F32):
            return stack.enter_context(nc.sbuf_tensor(name, shape, dt))

        def sem(name):
            return stack.enter_context(nc.semaphore(name))

        def sems(name, n):
            return [sem(f"{name}{i}") for i in range(n)]

        banks = [stack.enter_context(nc.psum_tensor(f"bank{i}", [P, 512], F32)) for i in range(8)]
        score_ps = banks[0:4]
        q_ps, k_ps, v_ps, o_ps = score_ps
        up_ps = banks[4]
        mix_ps = banks[5]
        tr_a, tr_b = banks[6:8]

        ident = sb("ident", [P, P])
        ident_b = sb("ident_b", [P, P], BF16)
        ones_col = sb("ones_col", [P, 1])
        minus_half = sb("minus_half", [P, 2])
        group_mean = sb("group_mean", [P, P], BF16)
        gain_in = sb("gain_in", [P, 2])
        gain = sb("gain", [P, 2])
        w_hi = [sb(f"w{n}_hi", [P, C, D], F16) for n in "qkvo"]
        w_lo = [sb(f"w{n}_lo", [P, C, D], F16) for n in "qkvo"]
        w_top = sb("w_top", [P, 4])
        w_top_all = sb("w_top_all", [P, 4])
        w_step = sb("w_step", [P, 4])
        w_scale = sb("w_scale", [P, 4])
        w1 = sb("w1", [P, C, HID], BF16)
        w2 = sb("w2", [P, M, D], BF16)
        qb_sb = sb("qb_sb", [P, D])
        kb_sb = sb("kb_sb", [P, D])
        qk_norm = sb("qk_norm", [P, D])
        o_const = sb("o_const", [P, D])
        vb_col = sb("vb_col", [P, C])
        qk_top = sb("qk_top", [P, 1])
        qk_inv = sb("qk_inv", [P, 1])
        exp_scale = sb("exp_scale", [P, 1])
        neg_exp_scale = sb("neg_exp_scale", [P, 1])
        q_unscale = sb("q_unscale", [P, 1])
        k_unscale0 = sb("k_unscale0", [P, 1])
        o_unscale0 = sb("o_unscale0", [P, 1])
        scale_top = sb("scale_top", [P, NU])
        fc_top = sb("fc_top", [P, 1])
        fc_top_all = sb("fc_top_all", [P, 1])
        relu_scale = sb("relu_scale", [P, 1])
        h_unscale = sb("h_unscale", [P, 1])
        ms_scale = sb("ms_scale", [P, 1])
        out_gain = sb("out_gain", [P, 1])
        tmp_c = sb("tmp_c", [P, 4])

        x_sb = [sb(f"x_sb{i}", [P, D]) for i in range(4)]
        ctx_sb = [sb(f"ctx_sb{i}", [P, D]) for i in range(2)]
        ln1_raw = sb("ln1_raw", [P, 6])
        ln1_mv = sb("ln1_mv", [P, 2])
        ln1_in = sb("ln1_in", [P, 2])
        ln1_rstd = sb("ln1_rstd", [P, 1])
        xn = sb("xn", [P, D])
        xt_hi = sb("xt_hi", [P, D], F16)
        xt_lo = sb("xt_lo", [P, D], F16)
        ctx_part = sb("ctx_part", [P, 1], BF16)
        ctx_top = sb("ctx_top", [P, 1])
        ctx_top0 = sb("ctx_top0", [P, 1])
        ctx_step = sb("ctx_step", [P, 1])
        ctx_scale = sb("ctx_scale", [P, 1])
        k_unscale = sb("k_unscale", [P, 1])
        o_unscale = [sb(f"o_unscale_t{i}", [P, 1]) for i in range(2)]
        ct_hi = sb("ct_hi", [P, D], F16)
        ct_lo = sb("ct_lo", [P, D], F16)
        q_raw = sb("q_raw", [P, D])
        k_raw = sb("k_raw", [P, D])
        square_out = [sb(f"square_out{i}", [P, D], BF16) for i in range(2)]
        q_ss = sb("q_ss", [P, 1])
        k_ss = sb("k_ss", [P, 1])
        q_ms = sb("q_ms", [P, 1])
        k_ms = sb("k_ms", [P, 1])
        q_rms = sb("q_rms", [P, 1])
        k_rms = sb("k_rms", [P, 1])
        qn = sb("qn", [P, D])
        kn = sb("kn", [P, D])
        qt_hi = sb("qt_hi", [P, D], F16)
        qt_lo = sb("qt_lo", [P, D], F16)
        kt_hi = sb("kt_hi", [P, D], F16)
        kt_lo = sb("kt_lo", [P, D], F16)
        v_hi = sb("v_hi", [P, D], F16)
        v_lo = sb("v_lo", [P, D], F16)
        s_top = sb("s_top", [P, H])
        exp_bias = sb("exp_bias", [P, H])
        p_sum = sb("p_sum", [P, H])
        p_inv = sb("p_inv", [P, H])
        p_sb = [sb(f"p_sb{i}", [P, 512]) for i in range(4)]
        pt_hi = [sb(f"pt_hi{i}", [P, 512], F16) for i in range(2)]
        pt_lo = [sb(f"pt_lo{i}", [P, 512], F16) for i in range(2)]
        attn = sb("attn", [P, D])
        at_hi = sb("at_hi", [P, D], F16)
        at_lo = sb("at_lo", [P, D], F16)
        xb = sb("xb", [P, D])
        x1 = [sb(f"x1_{j}", [P, D]) for j in range(LAG)]
        ln2_raw = sb("ln2_raw", [P, 6])
        ln2_mv = sb("ln2_mv", [P, 2])
        ln2_in = sb("ln2_in", [P, 2])
        ln2_rstd = sb("ln2_rstd", [P, 1])
        x1n = sb("x1n", [P, D])
        ft_hi = [sb(f"ft_hi{i}", [P, C, R], F16) for i in range(2)]
        ft_lo = [sb(f"ft_lo{i}", [P, C, R], F16) for i in range(2)]
        relu_sb = [sb(f"relu_sb{i}", [P, 512]) for i in range(2)]
        h_sb = [sb(f"h_sb{i}", [P, 512]) for i in range(2)]
        hh_sb = [sb(f"hh_sb{i}", [P, 512]) for i in range(2)]
        hh_sum = sb("hh_sum", [P, 512])
        h_ms = sb("h_ms", [P, 2])
        h_rms = sb("h_rms", [P, 2])
        h_gain = sb("h_gain", [P, 2])
        out_sb = [sb(f"out_sb{i}", [P, D]) for i in range(2)]
        big = sb("big", [P, 4 * C * 512])
        stage = [big[:, s * 2048:(s + 1) * 2048] for s in range(4)]
        ht_hi, ht_lo = ([big[:, o + 4096 * i:o + 4096 * i + 2048].bitcast(F16) for i in range(2)] for o in (0, 2048))
        before_out = [out_sb[i // 2][:, i % 2 * 256:(i % 2 + 1) * 256].bitcast(BF16) for i in range(4)]
        abs_w = [sb(f"abs_w{i}", [P, 512], BF16)[:, :] for i in range(TABS - 2)] + before_out[0:2]
        t_scale = [sb(f"t_scale{i}", [P, 512], BF16)[:, :] for i in range(TD - 1)] + before_out[2:3]
        t_mask = [sb(f"t_mask{i}", [P, 512], BF16)[:, :] for i in range(TD - 1)] + before_out[3:4]
        vb_wide = x1[0][:, :].rearrange("p (c k) -> p c k", c=C)
        ob_in = x1[1]
        nk_in = x1[2]

        consts_ready = sem("consts_ready")
        zeros_ready, ident_ready = sem("zeros_ready"), sem("ident_ready")
        small_in = sem("small_in")
        stage_in = sems("stage_in", 4)
        w_top_part, w_top_spread, w_top_ready, w_scale_ready, w_hi_ready = (
            sem(n) for n in ("w_top_part", "w_top_spread", "w_top_ready", "w_scale_ready", "w_hi_ready"))
        w_lo_ready = sems("w_lo_ready", 4)
        w_step_ready = sem("w_step_ready")
        norms_ready = sem("norms_ready")
        gain_ready, vb_ready, wov_done, setup_dve = (sem(n) for n in ("gain_ready", "vb_ready", "wov_done", "setup_dve"))
        abs_ready, sign_ready, gsum_done, tscale_ready, tmask_ready, tsigned_ready, tern_ready = (
            sem(n) for n in ("abs_ready", "sign_ready", "gsum_done", "tscale_ready", "tmask_ready",
                             "tsigned_ready", "tern_ready"))
        fc_top_part, fc_top_spread, fc_top_ready, ffn_consts = (
            sem(n) for n in ("fc_top_part", "fc_top_spread", "fc_top_ready", "ffn_consts"))
        x_in = sems("x_in", 4)
        ctx_in = sems("ctx_in", 2)
        out_free = sems("out_free", 2)
        dve_step = sem("dve_step")
        ln1_ready, ln1_rstd_ready, xn_ready, xt_done, xhi_ready, xlo_ready = (
            sem(n) for n in ("ln1_ready", "ln1_rstd_ready", "xn_ready", "xt_done", "xhi_ready", "xlo_ready"))
        ctx_part_ready, ctx_spread, ctx_top_ready, ctx_step_ready, ctx_scale_ready, chi_ready, clo_ready = (
            sem(n) for n in ("ctx_part_ready", "ctx_spread", "ctx_top_ready", "ctx_step_ready", "ctx_scale_ready",
                             "chi_ready", "clo_ready"))
        q_done, k_done, v_done, o_done = (sem(n) for n in ("q_done", "k_done", "v_done", "o_done"))
        qraw_ready, kraw_ready, qss_ready, kss_ready = (
            sem(n) for n in ("qraw_ready", "kraw_ready", "qss_ready", "kss_ready"))
        qms_ready, qrms_ready, qn_ready, kms_ready, krms_ready, kn_ready = (
            sem(n) for n in ("qms_ready", "qrms_ready", "qn_ready", "kms_ready", "krms_ready", "kn_ready"))
        qt_done, kt_done, qhi_ready, qlo_ready, khi_ready, klo_ready, vhi_ready, vlo_ready = (
            sem(n) for n in ("qt_done", "kt_done", "qhi_ready", "qlo_ready", "khi_ready", "klo_ready", "vhi_ready",
                             "vlo_ready"))
        s_done = sem("s_done")
        top_ready, bias_ready, exp_ready, pt_done, phi_ready, plo_ready, pv_done = (
            sem(n) for n in ("top_ready", "bias_ready", "exp_ready", "pt_done", "phi_ready", "plo_ready", "pv_done"))
        pinv_ready, attn_ready, at_done, ahi_ready, alo_ready = (
            sem(n) for n in ("pinv_ready", "attn_ready", "at_done", "ahi_ready", "alo_ready"))
        xb_ready, x1_ready, ln2_ready, ln2_rstd_ready, x1n_ready, ft_done, fhi_ready, flo_ready = (
            sem(n) for n in ("xb_ready", "x1_ready", "ln2_ready", "ln2_rstd_ready", "x1n_ready", "ft_done", "fhi_ready",
                             "flo_ready"))
        up_done, relu_ready, hhi_ready, h_ready, hlo_ready, hh_ready, hsum_ready = (
            sem(n) for n in ("up_done", "relu_ready", "hhi_ready", "h_ready", "hlo_ready", "hh_ready", "hsum_ready"))
        hms_ready, hrms_ready, hgain_ready = (sem(n) for n in ("hms_ready", "hrms_ready", "hgain_ready"))
        hss_done = sem("hss_done")
        down_done, out_ready = (sem(n) for n in ("down_done", "out_ready"))

        block = stack.enter_context(nc.Block())

        def need(eng, s, n):
            if not isinstance(n, int) or n > 0:
                eng.wait_ge(s, n)

        def held(eng, n):
            if not isinstance(n, int):
                eng.compute_val(n)
            return n

        def piece(t, f):
            return UP * t - 2 * UP + f

        def pairs_before(g, j):
            return 2 * g + j // 2 - 1

        def last_slot(t):
            return isinstance(t, int) and t == NT - 1

        def units(t, place, tern):
            before = TERN * t + sum(PLACES[t][:place]) if tern else 0
            return range(before, before + PLACES[t][place]) if tern else ()

        def ternary_bank(n):
            if n < NU:
                return up_ps
            return mix_ps if n % TERN < sum(PLACES[n // TERN][:5]) else o_ps

        def ternary_place(n):
            if n < NU:
                return w1[:, n // 4, (n % 4) * 512:(n % 4 + 1) * 512]
            return w2[:, n - NU, :]

        def ternary_stage(b):
            return (b, 2) if b < 4 else (2 + b % 2, 3 + (b - 4) // 2)

        @block.sync
        def _(sp):
            def load_tile(t, b):
                need(sp, xb_ready, t - 3)
                sp.dma_start(x_sb[b][:, :], x[bass.ds(t, 1), :, :]).then_inc(x_in[b], 16)
                need(sp, clo_ready, t - 1)
                sp.dma_start(ctx_sb[b % 2][:, :], ctx_t[bass.ds(t, 1), :, :]).then_inc(ctx_in[b % 2], 16)

            def load_ternary(b):
                if b < 4:
                    sp.wait_ge(w_lo_ready[b], 1)
                    if b == 3:
                        sp.wait_ge(wov_done, 1)
                else:
                    sp.wait_ge(sign_ready, 4 * (b - 2) + 4)
                s = ternary_stage(b)[0]
                src = w_fc_t[:, b, :] if b < 4 else w_proj_t[:, (b - 4) * 4:(b - 3) * 4, :]
                sp.dma_start(stage[s], src).then_inc(stage_in[s], 16)

            def store(t, i):
                sp.wait_ge(out_ready, t + 1)
                sp.dma_start(out[bass.ds(t, 1), :, :], out_sb[i % 2][:, :]).then_inc(out_free[i % 2], 16)

            sp.dma_start(x_sb[0][:, :], x[0:1, :, :]).then_inc(x_in[0], 16)
            sp.dma_start(ctx_sb[0][:, :], ctx_t[0:1, :, :]).then_inc(ctx_in[0], 16)
            for s, w in enumerate((wq_t, wk_t, wv_t, wo_t)):
                sp.dma_start(stage[s], w).then_inc(stage_in[s], 16)
                if s == 1:
                    for dst, src in ((gain_in, gains), (qb_sb, q_b), (kb_sb, k_b), (qk_norm, norm_q), (nk_in, norm_k),
                                     (ob_in, o_b), (vb_col, v_b)):
                        sp.dma_start(dst[:, :], src).then_inc(small_in, 16)
                    load_tile(1, 1)
            load_ternary(0)
            load_ternary(1)
            load_tile(2, 2)
            load_ternary(2)
            load_ternary(3)
            load_tile(3, 3)
            load_tile(4, 0)
            load_ternary(4)
            load_ternary(5)
            load_tile(5, 1)
            load_ternary(6)
            load_ternary(7)
            load_tile(6, 2)

            def round_of(g):
                for j in range(J):
                    t = J * g + j
                    if not isinstance(t, int) or t + 3 < NT:
                        load_tile(t + 3, (j + 3) % 4)
                    store(t - LAG, j)

            with sp.Fori(1, NG - 1) as g:
                round_of(g)
            round_of(NG - 1)
            for i in range(LAG):
                store(NT - LAG + i, i)
            for i in range(2):
                sp.wait_ge(out_free[i], 16 * (NT // 2 + 1))

        @block.tensor
        def _(pe):
            def transpose4(dst, src, done):
                for c in range(C):
                    last = nc.tensor.transpose(dst[:, c * P:(c + 1) * P], src[:, c * P:(c + 1) * P], ident[:, :])
                last.then_inc(done, 1)

            def project(dst, hi, lo, w, done):
                for c in range(C):
                    col = slice(c * P, (c + 1) * P)
                    nc.tensor.matmul(dst[:, :], hi[:, col], w_hi[w][:, c, :], start=(c == 0), stop=False)
                    nc.tensor.matmul(dst[:, :], hi[:, col], w_lo[w][:, c, :], start=False, stop=False)
                    last = nc.tensor.matmul(dst[:, :], lo[:, col], w_hi[w][:, c, :], start=False, stop=(c == C - 1))
                last.then_inc(done, 1)

            def project_first(dst, hi, hi_ready, lo, lo_ready, w, done):
                pe.wait_ge(w_hi_ready, w + 1)
                for n, (rows, ready, weight) in enumerate(((hi, hi_ready, w_hi[w]), (lo, lo_ready, w_hi[w]),
                                                           (hi, w_lo_ready[w], w_lo[w]))):
                    pe.wait_ge(ready, 1)
                    for c in range(C):
                        last = nc.tensor.matmul(dst[:, :], rows[:, c * P:(c + 1) * P], weight[:, c, :],
                                                start=(n == 0 and c == 0), stop=(n == 2 and c == C - 1))
                last.then_inc(done, 1)

            def spread(dst, column, done, eye=ident):
                nc.tensor.matmul(dst[:, 0:P], column.to_broadcast([P, P]), eye[:, :], start=True, stop=True).then_inc(done, 1)

            def ffn_up(g, j, f, dst, banks=1):
                t, i, n = J * g + j, (j // 2 + 1) % 2, UP * (j % 2) + f
                if n == 0:
                    pe.wait_ge(flo_ready, t)
                    need(pe, hms_ready, pairs_before(g, j))
                need(pe, relu_ready, piece(t, f) - banks + 1)
                for u in range(2):
                    m = 2 * n + u
                    half = slice(u * R, (u + 1) * R)
                    for c in range(C):
                        w = w1[:, c, m * P:(m + 1) * P]
                        nc.tensor.matmul(dst[:, half], w, ft_hi[i][:, c, :], start=(c == 0), stop=False)
                        last = nc.tensor.matmul(dst[:, half], w, ft_lo[i][:, c, :], start=False, stop=(c == C - 1))
                last.then_inc(up_done, 1)

            def ffn_down(g, j, p, dst, waits=1):
                i, sums = j // 2, j % 2 == 0 and p == (3 if waits == 4 else 1)
                if j % 2 == 0 and (p == 0 or waits == 4):
                    n = 2 * (3 - p) if waits == 4 else 0
                    pe.wait_ge(hlo_ready, piece(J * g + j, 0) - n)
                if j == 0 and p == 1:
                    pe.wait_ge(tern_ready, 2 * NU)
                elif j == 0 and p == 0:
                    pe.wait_ge(tern_ready, NU + NU // 4)
                if sums:
                    pe.wait_ge(hsum_ready, 2 * UP * pairs_before(g, j))
                    pe.wait_ge(relu_ready, piece(J * g + j, 0))
                for m in range(4 * p, 4 * p + 4):
                    row = slice(m * R + j % 2 * P, m * R + j % 2 * P + P)
                    nc.tensor.matmul(dst[:, :], ht_hi[i][:, row], w2[:, m, :], start=(m == 0), stop=False)
                    last = nc.tensor.matmul(dst[:, :], ht_lo[i][:, row], w2[:, m, :], start=False, stop=(m == M - 1))
                    if p == 3 and m == M - 1:
                        last.then_inc(down_done, 1)
                    if sums and m % 2:
                        square_sum(m % 4 // 2).then_inc(hss_done, 1)

            def square_sum(i):
                return nc.tensor.matmul(up_ps[:, i:i + 1], hh_sum[:, i * P:(i + 1) * P], ones_col[:, :], start=True, stop=True)

            def ternary(n):
                pe.wait_ge(abs_ready, n + 1)
                need(pe, tscale_ready, n)
                if ternary_bank(n) is o_ps:
                    pe.wait_ge(exp_ready, 4 * (n // TERN) + 4)
                nc.tensor.matmul(ternary_bank(n)[:, :], group_mean[:, :], abs_w[n % TABS], start=True, stop=True).then_inc(gsum_done, 1)

            def normed_rows(t, dst):
                pe.wait_ge(x1n_ready, t + 1)
                transpose4(dst, x1n, ft_done)

            def values_of(t, b):
                pe.wait_ge(plo_ready, 4 * t + b + 1)
                for u in range(4):
                    h = slice((4 * u + b) * HD, (4 * u + b + 1) * HD)
                    q = slice(u * P, (u + 1) * P)
                    nc.tensor.matmul(mix_ps[:, h], pt_hi[b % 2][:, q], v_hi[:, h], start=True, stop=False)
                    nc.tensor.matmul(mix_ps[:, h], pt_hi[b % 2][:, q], v_lo[:, h], start=False, stop=False)
                    last = nc.tensor.matmul(mix_ps[:, h], pt_lo[b % 2][:, q], v_hi[:, h], start=False, stop=True)
                last.then_inc(pv_done, 1)

            def probs_t(t, b):
                pe.wait_ge(exp_ready, 4 * t + b + 1)
                transpose4((tr_a, tr_b)[b % 2], p_sb[b], pt_done)

            def project_out(t, units_before=0):
                if isinstance(t, int) and t == 0:
                    pe.wait_ge(w_lo_ready[3], 1)
                if units_before:
                    pe.wait_ge(tscale_ready, units_before)
                pe.wait_ge(alo_ready, t + 1)
                project(o_ps, at_hi, at_lo, 3, o_done)

            def spread_weight(s, dst):
                pe.wait_ge(w_top_part, s + 1)
                if s == 0:
                    pe.wait_ge(ctx_top_ready, 1)
                else:
                    pe.wait_ge(w_top_ready, s)
                spread(dst, w_top[:, s:s + 1], w_top_spread)

            def constant_row():
                pe.wait_ge(vb_ready, 1)
                pe.wait_ge(stage_in[3], 16)
                for c in range(C):
                    last = nc.tensor.matmul(mix_ps[:, :], vb_wide[:, c, :], stage[3][:, c * D:(c + 1) * D], start=(c == 0),
                                            stop=(c == C - 1))
                last.then_inc(wov_done, 1)

            def slot(g, j, tern, up, down):
                t = J * g + j
                more, first = not last_slot(t), isinstance(t, int) and t == 0
                pe.wait_ge(qn_ready, t + 1)
                if first:
                    pe.wait_ge(xlo_ready, 1)
                else:
                    pe.wait_ge(alo_ready, t)
                transpose4(tr_a, qn, qt_done)
                if not first:
                    project_out(t - 1, 2 * NU if down and j == 0 else TERN * J - TERN if tern and j == 3 else 0)
                pe.wait_ge(kn_ready, t + 1)
                if more and not first:
                    pe.wait_ge(ctx_top_ready, t + 2)
                transpose4(tr_b, kn, kt_done)
                if first:
                    pe.wait_ge(w_top_ready, 4)
                    pe.wait_ge(ctx_part_ready, 2)
                    spread(up_ps[:, P:2 * P], ctx_part[:, :], ctx_spread, ident_b)
                if down:
                    ffn_down(g, j, 0, mix_ps)
                if tern and t == 2:
                    pe.wait_ge(fc_top_part, 1)
                    spread(up_ps, fc_top[:, :], fc_top_spread)
                for n in units(t, 0, tern):
                    ternary(n)
                if more:
                    pe.wait_ge(xn_ready, t + 2)
                    pe.wait_ge(qlo_ready, t + 1)
                    transpose4(tr_a, xn, xt_done)
                pe.wait_ge(qlo_ready, t + 1)
                pe.wait_ge(klo_ready, t + 1)
                pe.wait_ge(qraw_ready, t + 1)
                pe.wait_ge(kraw_ready, t + 1)
                pe.wait_ge(vlo_ready, t + 1)
                need(pe, x1_ready, t)
                for u in range(4):
                    col = slice(u * P, (u + 1) * P)
                    for n, (q, k) in enumerate(((qt_hi, kt_hi), (qt_hi, kt_lo), (qt_lo, kt_hi))):
                        for b in range(4):
                            row = slice(b * HD, (b + 1) * HD)
                            last = nc.tensor.matmul(score_ps[b][:, col], q[row, col], k[row, col], start=(n == 0),
                                                    stop=(n == 2))
                last.then_inc(s_done, 1)
                if first:
                    pe.wait_ge(ctx_top_ready, 2)
                if not tern:
                    normed_rows(t - 1, tr_b)
                for p in range(1, 4):
                    if down:
                        ffn_down(g, j, p, mix_ps)
                    for n in units(t, p, tern):
                        ternary(n)
                    if tern and not first and p == 1:
                        normed_rows(t - 1, tr_b)
                if more:
                    pe.wait_ge(xlo_ready, t + 2)
                probs_t(t, 0)
                for n in units(t, 4, tern):
                    ternary(n)
                if up:
                    if tern:
                        pe.wait_ge(tern_ready, NU)
                        pe.wait_ge(fc_top_ready, 1)
                    ffn_up(g, j, 0, up_ps)
                need(pe, flo_ready, t)
                probs_t(t, 1)
                if more:
                    project(q_ps, xt_hi, xt_lo, 0, q_done)
                else:
                    ffn_down(NG, 0, 0, q_ps, 4)
                if down:
                    pe.wait_ge(out_ready, t - LAG + 1)
                elif first:
                    pe.wait_ge(setup_dve, 1)
                elif up:
                    pe.wait_ge(tscale_ready, TERN * t + sum(PLACES[t][:5]))
                values_of(t, 0)
                probs_t(t, 2)
                values_of(t, 1)
                for n in units(t, 5, tern):
                    ternary(n)
                if up:
                    ffn_up(g, j, 1, up_ps)
                probs_t(t, 3)
                values_of(t, 2)
                if more:
                    pe.wait_ge(clo_ready, t + 2)
                    project(k_ps, ct_hi, ct_lo, 1, k_done)
                else:
                    ffn_down(NG, 0, 1, q_ps, 4)
                values_of(t, 3)
                for n in units(t, 6, tern):
                    ternary(n)
                if up:
                    ffn_up(g, j, 2, up_ps)
                if not (isinstance(t, int) and t + 2 >= NT):
                    pe.wait_ge(ctx_part_ready, t + 3)
                    spread(tr_b, ctx_part[:, :], ctx_spread, ident_b)
                pe.wait_ge(attn_ready, t + 1)
                transpose4(tr_a, attn, at_done)
                if more:
                    project(v_ps, ct_hi, ct_lo, 2, v_done)
                for n in units(t, 7, tern):
                    ternary(n)
                if up:
                    ffn_up(g, j, 3, up_ps)

            pe.wait_ge(consts_ready, 5)
            pe.wait_ge(ctx_part_ready, 1)
            spread(tr_b, ctx_part[:, :], ctx_spread, ident_b)
            pe.wait_ge(xn_ready, 1)
            transpose4(tr_a, xn, xt_done)
            spread_weight(0, tr_b)
            spread_weight(1, tr_b)
            project_first(q_ps, xt_hi, xhi_ready, xt_lo, xlo_ready, 0, q_done)
            spread_weight(2, tr_b)
            project_first(k_ps, ct_hi, chi_ready, ct_lo, clo_ready, 1, k_done)
            constant_row()
            project_first(v_ps, ct_hi, chi_ready, ct_lo, clo_ready, 2, v_done)
            spread_weight(3, up_ps)
            for j in range(J):
                slot(0, j, True, j >= 2, False)
            with pe.Fori(1, NG - 1) as g:
                for j in range(J):
                    slot(g, j, False, True, True)
            for j in range(J):
                slot(NG - 1, j, False, True, True)
            project_out(NT - 1)
            for p in range(2, 4):
                ffn_down(NG, 0, p, q_ps, 4)
            pe.wait_ge(klo_ready, NT)
            normed_rows(NT - 1, tr_b)
            for p in range(4):
                ffn_down(NG, 1, p, tr_a)
            pe.wait_ge(out_ready, NT - 3)
            for j in range(2):
                for f in range(UP):
                    ffn_up(NG, j, f, score_ps[f], 4)
            for p in range(4):
                ffn_down(NG, 2, p, mix_ps, 4)
            pe.wait_ge(out_ready, NT - 2)
            for p in range(4):
                ffn_down(NG, 3, p, tr_a)

        @block.scalar
        def _(act):
            def copy_hi(dst, src, done, scale=1.0):
                nc.scalar.activation(dst, src, ACT.Copy, scale=scale).then_inc(done, 1)

            def x_hi(t):
                act.wait_ge(xt_done, t + 1)
                need(act, q_done, t)
                copy_hi(xt_hi[:, :], tr_a[:, :], xhi_ready)

            def context_hi(t, par):
                act.wait_ge(ctx_scale_ready, t + 1)
                need(act, v_done, t)
                nc.scalar.activation(ct_hi[:, :], ctx_sb[par][:, :], ACT.Identity,
                                     scale=ctx_scale[:, :]).then_inc(chi_ready, 1)

            def square_sum(t, raw, raw_ready, n, total, done):
                act.wait_ge(raw_ready, t + 1)
                need(act, done, t)
                nc.scalar.activation(square_out[n][:, :], raw[:, :], ACT.Square,
                                     accum_out=total[:, :]).then_inc(done, 1)

            def v_hi_of(t):
                act.wait_ge(v_done, t + 1)
                need(act, pv_done, 4 * t)
                copy_hi(v_hi[:, :], v_ps[:, :], vhi_ready, V_SCALE)

            def relu_hi(g, j, f, src):
                t = J * g + j
                k = piece(t, f)
                n = UP * (j % 2) + f
                act.wait_ge(up_done, k + 1)
                need(act, h_ready, k - 1)
                need(act, hhi_ready, k - 1)
                nc.scalar.activation(relu_sb[f % 2][:, :], src[:, :], ACT.Relu, scale=relu_scale[:, :]).then_inc(relu_ready, 1)
                act.wait_ge(relu_ready, k + 1)
                nc.scalar.activation(ht_hi[(j // 2 + 1) % 2][:, n * 512:(n + 1) * 512], relu_sb[f % 2][:, :],
                                     ACT.Square).then_inc(hhi_ready, 1)

            def squares(g, j, f):
                k, n = piece(J * g + j, f), UP * (j % 2) + f
                act.wait_ge(h_ready, k + 1)
                if n == 0:
                    need(act, hss_done, 2 * pairs_before(g, j))
                    dst = hh_sum
                else:
                    need(act, hsum_ready, 2 * UP * pairs_before(g, j) + max(0, n - 2))
                    dst = hh_sb[f % 2]
                nc.scalar.activation(dst[:, :], h_sb[f % 2][:, :], ACT.Square).then_inc(hh_ready, 1)

            def ternary(n):
                if n >= 2 * NU:
                    return
                s, loads = ternary_stage(n // 4)
                if n % 4 == 0:
                    act.wait_ge(stage_in[s], 16 * loads)
                src = stage[s][:, (n % 4) * 512:(n % 4 + 1) * 512]
                need(act, gsum_done, n - TABS + 1)
                need(act, tmask_ready, n - TABS + 1)
                nc.scalar.activation(abs_w[n % TABS], src, ACT.Abs, scale=2.0).then_inc(abs_ready, 1)
                nc.scalar.activation(ternary_place(n), src, ACT.Sign).then_inc(sign_ready, 1)

            def normed_hi(t, j):
                act.wait_ge(ft_done, t + 1)
                nc.scalar.activation(ft_hi[j // 2][:, :, j % 2 * P:(j % 2 + 1) * P],
                                     tr_b[:, :].rearrange("p (c t) -> p c t", c=C), ACT.Copy).then_inc(fhi_ready, 1)

            def exps(t, b):
                act.wait_ge(bias_ready, 4 * t + b + 1)
                need(act, pt_done, 4 * t + b - 3)
                if b == 0:
                    need(act, pinv_ready, t)
                for u in range(4):
                    h = 4 * u + b
                    last = nc.scalar.activation(p_sb[b][:, u * P:(u + 1) * P], score_ps[b][:, u * P:(u + 1) * P],
                                                ACT.Exp, scale=exp_scale[:, :], bias=exp_bias[:, h:h + 1],
                                                accum_out=p_sum[:, h:h + 1])
                last.then_inc(exp_ready, 1)

            def probs_hi(t, b):
                act.wait_ge(pt_done, 4 * t + b + 1)
                need(act, pv_done, 4 * t + b - 1)
                copy_hi(pt_hi[b % 2][:, :], (tr_a, tr_b)[b % 2][:, :], phi_ready)

            def weight_sum(s):
                act.wait_ge(stage_in[s], 16)
                nc.scalar.activation(w_lo[s][:, :, :].rearrange("p c n -> p (c n)"), stage[s], ACT.Abs,
                                     accum_out=w_top[:, s:s + 1]).then_inc(w_top_part, 1)

            def weight_hi(s):
                act.wait_ge(w_scale_ready, s + 1)
                nc.scalar.activation(w_hi[s][:, :, :].rearrange("p c n -> p (c n)"), stage[s], ACT.Identity,
                                     scale=w_scale[:, s:s + 1]).then_inc(w_hi_ready, 1)

            def slot(g, j, tern, up, down):
                t = J * g + j
                more, first = not last_slot(t), isinstance(t, int) and t == 0
                started = isinstance(t, int) and t == 2
                act.wait_ge(qt_done, t + 1)
                need(act, s_done, t)
                copy_hi(qt_hi[:, :], tr_a[:, :], qhi_ready)
                if up and not started:
                    squares(g, j - 1, 3)
                act.wait_ge(kt_done, t + 1)
                copy_hi(kt_hi[:, :], tr_b[:, :], khi_ready)
                if more and not first:
                    context_hi(t + 1, (j + 1) % 2)
                for n in units(t, 0, tern):
                    ternary(n + TAHEAD)
                if more:
                    x_hi(t + 1)
                if first:
                    weight_hi(3)
                    context_hi(1, 1)
                exps(t, 0)
                for n in units(t, 1, tern):
                    ternary(n + TAHEAD)
                exps(t, 1)
                if not first:
                    normed_hi(t - 1, (j - 1) % J)
                for n in units(t, 2, tern):
                    ternary(n + TAHEAD)
                exps(t, 2)
                probs_hi(t, 0)
                exps(t, 3)
                for n in units(t, 3, tern):
                    ternary(n + TAHEAD)
                probs_hi(t, 1)
                if up:
                    if started:
                        act.wait_ge(ffn_consts, 1)
                    relu_hi(g, j, 0, up_ps)
                    squares(g, j, 0)
                for n in units(t, 4, tern):
                    ternary(n + TAHEAD)
                probs_hi(t, 2)
                if more:
                    square_sum(t + 1, q_raw, qraw_ready, 0, q_ss, qss_ready)
                if up:
                    relu_hi(g, j, 1, up_ps)
                probs_hi(t, 3)
                if up:
                    squares(g, j, 1)
                for n in units(t, 5, tern):
                    ternary(n + TAHEAD)
                if more:
                    square_sum(t + 1, k_raw, kraw_ready, 1, k_ss, kss_ready)
                if up:
                    relu_hi(g, j, 2, up_ps)
                for n in units(t, 6, tern):
                    ternary(n + TAHEAD)
                act.wait_ge(at_done, t + 1)
                need(act, o_done, t)
                copy_hi(at_hi[:, :], tr_a[:, :], ahi_ready)
                if up:
                    squares(g, j, 2)
                if more:
                    v_hi_of(t + 1)
                if up:
                    relu_hi(g, j, 3, up_ps)
                for n in units(t, 7, tern):
                    ternary(n + TAHEAD)

            for s in range(3):
                weight_hi(s)
                if s == 0:
                    x_hi(0)
                    act.wait_ge(small_in, 16 * 7)
                    nc.scalar.activation(gain[:, :], gain_in[:, :], ACT.Tanh).then_inc(gain_ready, 1)
                if s == 1:
                    context_hi(0, 0)
            square_sum(0, q_raw, qraw_ready, 0, q_ss, qss_ready)
            weight_sum(3)
            square_sum(0, k_raw, kraw_ready, 1, k_ss, kss_ready)
            for n in range(TAHEAD):
                ternary(n)
            v_hi_of(0)
            for j in range(J):
                slot(0, j, True, j >= 2, False)
            with act.Fori(1, NG - 1) as g:
                for j in range(J):
                    slot(g, j, False, True, True)
            for j in range(J):
                slot(NG - 1, j, False, True, True)
            squares(NG - 1, J - 1, 3)
            normed_hi(NT - 1, J - 1)
            for j in range(2):
                for f in range(UP):
                    relu_hi(NG, j, f, score_ps[f])
                    if j or f:
                        squares(NG, j - (f == 0), (f - 1) % UP)
            squares(NG, 1, UP - 1)

        @block.vector
        def _(dve):
            def sub_lo(dst, src, hi, hi_ready, n, done):
                dve.wait_ge(hi_ready, n)
                nc.vector.tensor_tensor(dst, src, hi, ALU.subtract).then_inc(done, 1)

            def row_stats(src, raw, mv, pair, done, n):
                first = held(dve, 4 * n + 1)
                nc.vector.bn_stats(raw[:, :], src).then_inc(done, 1)
                dve.wait_ge(consts_ready, 5)
                dve.wait_ge(done, first)
                nc.vector.bn_aggr(mv[:, :], raw[:, :]).then_inc(done, 1)
                dve.wait_ge(done, 4 * n + 2)
                nc.vector.tensor_scalar(pair[:, 0:1], mv[:, 0:1], -1.0, None, ALU.mult).then_inc(done, 1)
                nc.vector.tensor_scalar(pair[:, 1:2], mv[:, 1:2], LN_EPS, X_SCALE ** -2, ALU.add,
                                        ALU.mult).then_inc(done, 1)

            def x_stats(t, b, times):
                dve.wait_ge(x_in[b], 16 * times)
                need(dve, xn_ready, t)
                row_stats(x_sb[b][:, :], ln1_raw, ln1_mv, ln1_in, ln1_ready, t)

            def context_max(t, par, times):
                dve.wait_ge(ctx_in[par], 16 * times)
                need(dve, ctx_spread, t)
                nc.vector.tensor_reduce(ctx_part[:, :], ctx_sb[par][:, :], AX.X, ALU.max,
                                        apply_absolute_value=True).then_inc(ctx_part_ready, 1)

            def context_top(t, spread=tr_b):
                dve.wait_ge(ctx_spread, t + 1)
                need(dve, ctx_step_ready, 3 * t)
                nc.vector.tensor_reduce(ctx_top[:, :], spread[:, 0:P], AX.X, ALU.max).then_inc(ctx_top_ready, 1)

            def output_scale(par, top):
                return nc.vector.tensor_scalar(o_unscale[par][:, :], top[:, :], TINY, o_unscale0[:, :], ALU.max, ALU.mult)

            def context_scale(t, par):
                dve.wait_ge(ctx_top_ready, t + 1)
                need(dve, chi_ready, t)
                need(dve, clo_ready, t)
                need(dve, kraw_ready, t)
                need(dve, x1_ready, t - 1)
                nc.vector.tensor_scalar(ctx_step[:, :], ctx_top[:, :], TINY, 1.0 / C_MAX, ALU.max,
                                        ALU.mult).then_inc(ctx_step_ready, 1)
                nc.vector.tensor_scalar(k_unscale[:, :], ctx_top[:, :], TINY, k_unscale0[:, :], ALU.max,
                                        ALU.mult).then_inc(ctx_step_ready, 1)
                if isinstance(t, int) and t == 0:
                    nc.vector.tensor_copy(ctx_top0[:, :], ctx_top[:, :]).then_inc(ctx_step_ready, 1)
                else:
                    output_scale(par, ctx_top).then_inc(ctx_step_ready, 1)
                dve.wait_ge(ctx_step_ready, 3 * t + 3)
                nc.vector.reciprocal(ctx_scale[:, :], ctx_step[:, :]).then_inc(ctx_scale_ready, 1)

            def x_lo(t):
                need(dve, q_done, t)
                sub_lo(xt_lo[:, :], tr_a[:, :], xt_hi[:, :], xhi_ready, t + 1, xlo_ready)

            def context_lo(t, par):
                dve.wait_ge(chi_ready, t + 1)
                dve.wait_ge(ctx_scale_ready, t + 1)
                need(dve, v_done, t)
                nc.vector.scalar_tensor_tensor(out=ct_lo[:, :], in0=ctx_sb[par][:, :], scalar=ctx_scale[:, :],
                                               in1=ct_hi[:, :], op0=ALU.mult, op1=ALU.subtract).then_inc(clo_ready, 1)

            def q_out(t):
                dve.wait_ge(q_done, t + 1)
                need(dve, qn_ready, t)
                nc.vector.scalar_tensor_tensor(out=q_raw[:, :], in0=q_ps[:, :], scalar=q_unscale[:, :], in1=qb_sb[:, :],
                                               op0=ALU.mult, op1=ALU.add).then_inc(qraw_ready, 1)

            def k_out(t):
                dve.wait_ge(k_done, t + 1)
                need(dve, kn_ready, t)
                nc.vector.scalar_tensor_tensor(out=k_raw[:, :], in0=k_ps[:, :], scalar=k_unscale[:, :], in1=kb_sb[:, :],
                                               op0=ALU.mult, op1=ALU.add).then_inc(kraw_ready, 1)

            def k_norm(t):
                dve.wait_ge(krms_ready, t + 1)
                need(dve, kt_done, t)
                nc.vector.scalar_tensor_tensor(out=kn[:, :], in0=k_raw[:, :], scalar=k_rms[:, :], in1=qk_norm[:, :],
                                               op0=ALU.mult, op1=ALU.mult).then_inc(kn_ready, 1)

            def v_lo_of(t):
                dve.wait_ge(vhi_ready, t + 1)
                need(dve, pv_done, 4 * t)
                nc.vector.scalar_tensor_tensor(out=v_lo[:, :], in0=v_ps[:, :], scalar=V_SCALE, in1=v_hi[:, :],
                                               op0=ALU.mult, op1=ALU.subtract).then_inc(vlo_ready, 1)

            def hidden(g, j, f):
                k = piece(J * g + j, f)
                dve.wait_ge(relu_ready, k + 1)
                need(dve, hh_ready, k - 1)
                need(dve, hlo_ready, k - 1)
                nc.vector.tensor_tensor(h_sb[f % 2][:, :], relu_sb[f % 2][:, :], relu_sb[f % 2][:, :],
                                        ALU.mult).then_inc(h_ready, 1)

            def hidden_lo(g, j, f):
                k = piece(J * g + j, f)
                n = UP * (j % 2) + f
                i = (j // 2 + 1) % 2
                dve.wait_ge(h_ready, k + 1)
                sub_lo(ht_lo[i][:, n * 512:(n + 1) * 512], h_sb[f % 2][:, :], ht_hi[i][:, n * 512:(n + 1) * 512], hhi_ready,
                       k + 1, hlo_ready)

            def ffn_out(g, j, src):
                dve.wait_ge(down_done, J * g + j - LAG + 1)
                dve.wait_ge(hgain_ready, pairs_before(g, j))
                if j == 0:
                    dve.wait_ge(tern_ready, 2 * NU)
                dve.wait_ge(out_free[j % 2], 16 * (2 * g - 1 + j // 2))
                nc.vector.scalar_tensor_tensor(out=out_sb[j % 2][:, :], in0=src[:, :], scalar=h_gain[:, j % 2:j % 2 + 1],
                                               in1=x1[j][:, :], op0=ALU.mult, op1=ALU.add).then_inc(out_ready, 1)

            def hidden_mean_square(g, j):
                n = pairs_before(g, j)
                dve.wait_ge(hss_done, 2 * n)
                nc.vector.tensor_scalar(h_ms[:, :], up_ps[:, 0:2], ms_scale[:, :], FFN_EPS, ALU.mult,
                                        ALU.add).then_inc(hms_ready, 1)

            def ternary(n):
                dve.wait_ge(gsum_done, n + 1)
                need(dve, tsigned_ready, n - TD + 1)
                if n < NU:
                    last = nc.vector.tensor_scalar(t_scale[n % TD], ternary_bank(n)[:, :], TERNARY_CLIP, None, ALU.max,
                                                   ALU.max, accum_out=scale_top[:, n:n + 1])
                else:
                    last = nc.vector.tensor_scalar(t_scale[n % TD], ternary_bank(n)[:, :], TERNARY_CLIP, None, ALU.max)
                last.then_inc(tscale_ready, 1)
                dve.wait_ge(tscale_ready, n + 1)
                need(dve, tern_ready, n - TD + 1)
                nc.vector.tensor_tensor(t_mask[n % TD], abs_w[n % TABS], t_scale[n % TD], ALU.is_gt).then_inc(tmask_ready, 1)

            def normed_lo(t, j):
                dve.wait_ge(fhi_ready, t + 1)
                col = slice(j % 2 * P, (j % 2 + 1) * P)
                nc.vector.tensor_tensor(ft_lo[j // 2][:, :, col], tr_b[:, :].rearrange("p (c t) -> p c t", c=C),
                                        ft_hi[j // 2][:, :, col], ALU.subtract).then_inc(flo_ready, 1)

            def score_top(t, b):
                if b == 0:
                    dve.wait_ge(s_done, t + 1)
                    need(dve, exp_ready, 4 * t)
                nc.vector.tensor_reduce(s_top[:, b:H:4], score_ps[b][:, :].rearrange("p (u k) -> p u k", k=P), AX.X,
                                        ALU.max).then_inc(top_ready, 1)
                dve.wait_ge(top_ready, 4 * t + b + 1)
                nc.vector.tensor_scalar(exp_bias[:, b:H:4], s_top[:, b:H:4], neg_exp_scale[:, :], LOG_P_SCALE, ALU.mult,
                                        ALU.add).then_inc(bias_ready, 1)

            def probs_lo(t, b):
                need(dve, pv_done, 4 * t + b - 1)
                sub_lo(pt_lo[b % 2][:, :], (tr_a, tr_b)[b % 2][:, :], pt_hi[b % 2][:, :], phi_ready, 4 * t + b + 1, plo_ready)

            def x1_out(t, j):
                dve.wait_ge(o_done, t + 1)
                dve.wait_ge(xb_ready, t + 1)
                nc.vector.scalar_tensor_tensor(out=x1[j][:, :], in0=o_ps[:, :], scalar=o_unscale[j % 2][:, :], in1=xb[:, :],
                                               op0=ALU.mult, op1=ALU.add).then_inc(x1_ready, 1)

            def x1_stats(t, j):
                dve.wait_ge(x1_ready, t + 1)
                need(dve, x1n_ready, t)
                row_stats(x1[j][:, :], ln2_raw, ln2_mv, ln2_in, ln2_ready, t)

            def attention(t):
                dve.wait_ge(pv_done, 4 * t + 4)
                dve.wait_ge(pinv_ready, t + 1)
                need(dve, at_done, t)
                nc.vector.tensor_tensor(attn[:, :].rearrange("p (h d) -> p h d", d=HD),
                                        mix_ps[:, :].rearrange("p (h d) -> p h d", d=HD),
                                        p_inv[:, :].unsqueeze(2).to_broadcast([P, H, HD]), ALU.mult).then_inc(attn_ready, 1)

            step = [0]

            def chain(ins):
                step[0] += 1
                ins.then_inc(dve_step, 1)
                dve.wait_ge(dve_step, step[0])

            def weight_max(s):
                dve.wait_ge(stage_in[s], 16)
                nc.vector.tensor_reduce(w_top[:, s:s + 1], stage[s], AX.X, ALU.max,
                                        apply_absolute_value=True).then_inc(w_top_part, 1)

            def weight_scale(s, spread):
                dve.wait_ge(w_top_spread, s + 1)
                nc.vector.tensor_reduce(w_top_all[:, s:s + 1], spread[:, 0:P], AX.X, ALU.max).then_inc(w_top_ready, 1)
                dve.wait_ge(w_top_ready, s + 1)
                nc.vector.tensor_scalar(w_step[:, s:s + 1], w_top_all[:, s:s + 1], TINY, 1.0 / (W_MAX if s < 3 else W_SUM), ALU.max,
                                        ALU.mult).then_inc(w_step_ready, 1)
                dve.wait_ge(w_step_ready, s + 1)
                nc.vector.reciprocal(w_scale[:, s:s + 1], w_step[:, s:s + 1]).then_inc(w_scale_ready, 1)

            def weight_lo(s):
                dve.wait_ge(w_scale_ready, s + 1)
                dve.wait_ge(w_hi_ready, s + 1)
                nc.vector.scalar_tensor_tensor(out=w_lo[s][:, :, :].rearrange("p c n -> p (c n)"), in0=stage[s],
                                               scalar=w_scale[:, s:s + 1],
                                               in1=w_hi[s][:, :, :].rearrange("p c n -> p (c n)"), op0=ALU.mult,
                                               op1=ALU.subtract).then_inc(w_lo_ready[s], 1)

            def output_constants():
                dve.wait_ge(gain_ready, 1)
                chain(nc.vector.tensor_tensor(tmp_c[:, 0:1], w_step[:, 2:3], w_step[:, 3:4], ALU.mult))
                chain(nc.vector.tensor_scalar(o_unscale0[:, :], tmp_c[:, 0:1], gain[:, 0:1], 1.0 / (V_SCALE * C_MAX), ALU.mult,
                                              ALU.mult))
                chain(output_scale(0, ctx_top0))

            def constant_row():
                dve.wait_ge(wov_done, 1)
                chain(nc.vector.tensor_tensor(o_const[:, :], mix_ps[:, :], ob_in[:, :], ALU.add))
                chain(nc.vector.tensor_scalar(o_const[:, :], o_const[:, :], gain[:, 0:1], None, ALU.mult))
                nc.vector.memset(tmp_c[:, 2:3], 0.0).then_inc(setup_dve, 1)

            def next_stats(t, g, j):
                x_stats(t, j % 4, g + 1 + j // J)
                context_max(t, j % 2, 2 * g + 1 + j // 2)

            def ffn_scales():
                dve.wait_ge(fc_top_spread, 1)
                nc.vector.tensor_reduce(fc_top_all[:, :], up_ps[:, 0:P], AX.X, ALU.max).then_inc(fc_top_ready, 1)
                dve.wait_ge(fc_top_ready, 1)
                chain(nc.vector.tensor_scalar(tmp_c[:, 1:2], fc_top_all[:, :], D * X_SCALE / R_MAX, None, ALU.mult))
                chain(nc.vector.reciprocal(relu_scale[:, :], tmp_c[:, 1:2]))
                chain(nc.vector.tensor_scalar(tmp_c[:, 1:2], fc_top_all[:, :], D / R_MAX, None, ALU.mult))
                chain(nc.vector.tensor_tensor(h_unscale[:, :], tmp_c[:, 1:2], tmp_c[:, 1:2], ALU.mult))
                chain(nc.vector.tensor_tensor(tmp_c[:, 0:1], h_unscale[:, :], h_unscale[:, :], ALU.mult))
                chain(nc.vector.tensor_scalar(ms_scale[:, :], tmp_c[:, 0:1], 1.0 / HID, None, ALU.mult))
                nc.vector.tensor_tensor(out_gain[:, :], h_unscale[:, :], gain[:, 1:2], ALU.mult).then_inc(ffn_consts, 1)

            def slot(g, j, tern, up, down):
                t = J * g + j
                more, first = not last_slot(t), isinstance(t, int) and t == 0
                started = isinstance(t, int) and t == 2
                two_more = not (isinstance(t, int) and t + 2 >= NT)
                need(dve, s_done, t)
                sub_lo(qt_lo[:, :], tr_a[:, :], qt_hi[:, :], qhi_ready, t + 1, qlo_ready)
                if up and not started:
                    hidden_lo(g, j - 1, 3)
                if not first:
                    x1_out(t - 1, (j - 1) % J)
                sub_lo(kt_lo[:, :], tr_b[:, :], kt_hi[:, :], khi_ready, t + 1, klo_ready)
                for n in units(t, 0, tern):
                    ternary(n)
                if first:
                    x_lo(1)
                    output_constants()
                    constant_row()
                    context_top(1, up_ps[:, P:2 * P])
                if more:
                    context_scale(t + 1, (j + 1) % 2)
                if not first:
                    x1_stats(t - 1, (j - 1) % J)
                if more:
                    if not first:
                        context_lo(t + 1, (j + 1) % 2)
                        x_lo(t + 1)
                for b in range(4):
                    score_top(t, b)
                    for n in units(t, b, tern and b > 0):
                        ternary(n)
                if first:
                    context_lo(1, 1)
                if down and j % 2 == 0:
                    hidden_mean_square(g, j)
                if two_more and not tern:
                    next_stats(t + 2, g, j + 2)
                if not first:
                    normed_lo(t - 1, (j - 1) % J)
                if started:
                    ffn_scales()
                if down:
                    ffn_out(g, j, mix_ps)
                for n in units(t, 4, tern):
                    ternary(n)
                probs_lo(t, 0)
                if two_more and tern:
                    next_stats(t + 2, g, j + 2)
                probs_lo(t, 1)
                if up:
                    hidden(g, j, 0)
                    hidden_lo(g, j, 0)
                if more:
                    q_out(t + 1)
                probs_lo(t, 2)
                for n in units(t, 5, tern):
                    ternary(n)
                if up:
                    hidden(g, j, 1)
                probs_lo(t, 3)
                if up:
                    hidden_lo(g, j, 1)
                dve.wait_ge(exp_ready, 4 * t + 4)
                need(dve, attn_ready, t)
                nc.vector.reciprocal(p_inv[:, :], p_sum[:, :]).then_inc(pinv_ready, 1)
                if first:
                    weight_lo(3)
                if more:
                    k_out(t + 1)
                attention(t)
                for n in units(t, 6, tern):
                    ternary(n)
                if more:
                    k_norm(t + 1)
                if up:
                    hidden(g, j, 2)
                    hidden_lo(g, j, 2)
                if two_more:
                    context_top(t + 2)
                need(dve, o_done, t)
                sub_lo(at_lo[:, :], tr_a[:, :], at_hi[:, :], ahi_ready, t + 1, alo_ready)
                for n in units(t, 7, tern):
                    ternary(n)
                if more:
                    v_lo_of(t + 1)
                if up:
                    hidden(g, j, 3)
                if isinstance(t, int) and t == 1:
                    dve.wait_ge(tscale_ready, NU)
                    nc.vector.tensor_reduce(fc_top[:, :], scale_top[:, :], AX.X, ALU.max).then_inc(fc_top_part, 1)

            nc.vector.memset(ones_col[:, :], 1.0).then_inc(consts_ready, 1)
            nc.vector.memset(minus_half[:, :], -0.5).then_inc(consts_ready, 1)
            chain(nc.vector.memset(group_mean[:, :], 0.0))
            for r in range(0, P, GROUP):
                nc.vector.memset(group_mean[r:r + GROUP, r:r + GROUP], 0.5 / GROUP).then_inc(consts_ready, 1)
            for i in range(2):
                nc.vector.memset(tmp_c[:, i:i + 1], 0.0).then_inc(out_free[i], 16)
            dve.wait_ge(consts_ready, 5)
            x_stats(0, 0, 1)
            context_max(0, 0, 1)
            context_top(0)
            weight_max(0)
            weight_scale(0, tr_b)
            weight_max(1)
            x_lo(0)
            weight_scale(1, tr_b)
            chain(nc.vector.tensor_scalar(k_unscale0[:, :], w_step[:, 1:2], 1.0 / C_MAX, None, ALU.mult))
            context_scale(0, 0)
            chain(nc.vector.tensor_scalar(q_unscale[:, :], w_step[:, 0:1], 1.0 / X_SCALE, None, ALU.mult))
            weight_lo(0)
            context_lo(0, 0)
            weight_max(2)
            dve.wait_ge(small_in, 16 * 7)
            chain(nc.vector.tensor_copy(vb_wide, vb_col[:, :].unsqueeze(2).to_broadcast([P, C, P])))
            nc.vector.memset(tmp_c[:, 3:4], 0.0).then_inc(vb_ready, 1)
            q_out(0)
            weight_scale(2, tr_b)
            weight_lo(1)
            weight_lo(2)
            k_out(0)
            dve.wait_ge(norms_ready, 1)
            chain(nc.vector.tensor_reduce(qk_top[:, :], qk_norm[:, :], AX.X, ALU.max, apply_absolute_value=True))
            chain(nc.vector.tensor_scalar(qk_top[:, :], qk_top[:, :], TINY, None, ALU.max))
            chain(nc.vector.reciprocal(qk_inv[:, :], qk_top[:, :]))
            chain(nc.vector.tensor_scalar(qk_norm[:, :], qk_norm[:, :], qk_inv[:, :], QK_SCALE, ALU.mult, ALU.mult))
            unit = float(HD) ** -0.5 / QK_SCALE ** 2
            chain(nc.vector.tensor_scalar(exp_scale[:, :], qk_top[:, :], unit, None, ALU.mult))
            chain(nc.vector.tensor_scalar(neg_exp_scale[:, :], qk_top[:, :], -unit, None, ALU.mult))
            k_norm(0)
            x_stats(1, 1, 1)
            context_max(1, 1, 1)
            weight_scale(3, up_ps)
            v_lo_of(0)
            for j in range(J):
                slot(0, j, True, j >= 2, False)
            with dve.Fori(1, NG - 1) as g:
                for j in range(J):
                    slot(g, j, False, True, True)
            for j in range(J):
                slot(NG - 1, j, False, True, True)
            hidden_lo(NG - 1, J - 1, 3)
            x1_out(NT - 1, J - 1)
            x1_stats(NT - 1, J - 1)
            hidden_mean_square(NG, 0)
            ffn_out(NG, 0, q_ps)
            normed_lo(NT - 1, J - 1)
            ffn_out(NG, 1, tr_a)
            for j in range(2):
                for f in range(UP):
                    hidden(NG, j, f)
                    hidden_lo(NG, j, f)
            hidden_mean_square(NG, 2)
            ffn_out(NG, 2, mix_ps)
            ffn_out(NG, 3, tr_a)

        @block.gpsimd
        def _(pool):
            def norm_rows(t, src, pair, pair_ready, rstd, rstd_ready, dst, done):
                count = held(pool, t + 1)
                if isinstance(t, int) and t == 0:
                    pool.wait_ge(consts_ready, 5)
                pool.wait_ge(pair_ready, 4 * t + 4)
                need(pool, done, t)
                nc.gpsimd.tensor_tensor(rstd[:, :], pair[:, 1:2], minus_half[:, 0:1], ALU.pow).then_inc(rstd_ready, 1)
                pool.wait_ge(consts_ready, 5)
                pool.wait_ge(rstd_ready, count)
                nc.gpsimd.tensor_scalar(dst, src, pair[:, 0:1], rstd[:, :], ALU.add, ALU.mult).then_inc(done, 1)

            def rms(t, ss, ss_ready, ms, ms_ready, scale, out_rms, done, used):
                count, before = held(pool, t + 1), held(pool, t)
                pool.wait_ge(consts_ready, 5)
                pool.wait_ge(ss_ready, count)
                need(pool, used, before)
                nc.gpsimd.tensor_scalar(ms[:, :], ss[:, :], scale ** -2 / D, QK_EPS * scale ** -2, ALU.mult,
                                        ALU.add).then_inc(ms_ready, 1)
                pool.wait_ge(ms_ready, count)
                nc.gpsimd.tensor_tensor(out_rms[:, :], ms[:, :], minus_half[:, 0:1], ALU.pow).then_inc(done, 1)

            def x_norm(t, b):
                need(pool, xt_done, t)
                norm_rows(t, x_sb[b][:, :], ln1_in, ln1_ready, ln1_rstd, ln1_rstd_ready, xn[:, :], xn_ready)

            def q_norm(t):
                rms(t, q_ss, qss_ready, q_ms, qms_ready, QK_SCALE, q_rms, qrms_ready, qn_ready)
                count, before = held(pool, t + 1), held(pool, t)
                pool.wait_ge(consts_ready, 5)
                pool.wait_ge(qrms_ready, count)
                need(pool, qt_done, before)
                nc.gpsimd.tensor_scalar(qn[:, :], q_raw[:, :], q_rms[:, :], 1.0, ALU.mult, ALU.mult).then_inc(qn_ready, 1)

            def k_rms_of(t):
                rms(t, k_ss, kss_ready, k_ms, kms_ready, 1.0, k_rms, krms_ready, kn_ready)

            def hidden_sum(g, j, f):
                n = UP * (j % 2) + f
                if n == 0:
                    return
                pool.wait_ge(hh_ready, piece(J * g + j, f) + 1)
                need(pool, hsum_ready, 2 * UP * pairs_before(g, j) + n - 1)
                nc.gpsimd.tensor_tensor(hh_sum[:, :], hh_sum[:, :], hh_sb[f % 2][:, :], ALU.add).then_inc(hsum_ready, 1)
                if n == 2 * UP - 1:
                    pool.wait_ge(hsum_ready, 2 * UP * pairs_before(g, j) + n)
                    nc.gpsimd.tensor_tensor(hh_sum[:, 0:R], hh_sum[:, 0:R], hh_sum[:, R:2 * R], ALU.add).then_inc(hsum_ready, 1)

            def hidden_gain(g, j):
                n = held(pool, pairs_before(g, j))
                t = J * g + j
                pool.wait_ge(hms_ready, n)
                nc.gpsimd.tensor_tensor(h_rms[:, :], h_ms[:, :], minus_half[:, :], ALU.pow).then_inc(hrms_ready, 1)
                pool.wait_ge(consts_ready, 5)
                pool.wait_ge(hrms_ready, n)
                nc.gpsimd.tensor_scalar(h_gain[:, :], h_rms[:, :], out_gain[:, :], 1.0, ALU.mult,
                                        ALU.mult).then_inc(hgain_ready, 1)

            def ternary(n):
                pool.wait_ge(sign_ready, n + 1)
                pool.wait_ge(tscale_ready, n + 1)
                nc.gpsimd.tensor_tensor(ternary_place(n), ternary_place(n), t_scale[n % TD], ALU.mult).then_inc(tsigned_ready, 1)
                pool.wait_ge(tsigned_ready, n + 1)
                pool.wait_ge(tmask_ready, n + 1)
                nc.gpsimd.tensor_tensor(ternary_place(n), ternary_place(n), t_mask[n % TD], ALU.mult).then_inc(tern_ready, 1)

            def x1_norm(t, j):
                need(pool, ft_done, t)
                norm_rows(t, x1[j][:, :], ln2_in, ln2_ready, ln2_rstd, ln2_rstd_ready, x1n[:, :], x1n_ready)

            def rows_plus_constant(t, j):
                need(pool, x1_ready, t)
                nc.gpsimd.tensor_tensor(xb[:, :], x_sb[j][:, :], o_const[:, :], ALU.add).then_inc(xb_ready, 1)

            def slot(g, j, tern, up, down):
                t = J * g + j
                more, first = not last_slot(t), isinstance(t, int) and t == 0
                started = isinstance(t, int) and t == 2
                if up and not started:
                    hidden_sum(g, j - 1, 3)
                if not first:
                    x1_norm(t - 1, (j - 1) % J)
                if not first:
                    rows_plus_constant(t, j)
                for n in units(t, 0, tern):
                    ternary(n)
                if down and j % 2 == 0:
                    hidden_gain(g, j)
                for p in range(1, 4):
                    for n in units(t, p, tern):
                        ternary(n)
                if not (isinstance(t, int) and t + 2 >= NT):
                    x_norm(t + 2, (j + 2) % 4)
                for p in range(4, 6):
                    for n in units(t, p, tern):
                        ternary(n)
                if up:
                    hidden_sum(g, j, 0)
                if more:
                    q_norm(t + 1)
                if up:
                    hidden_sum(g, j, 1)
                if more:
                    k_rms_of(t + 1)
                if first:
                    pool.wait_ge(setup_dve, 1)
                    rows_plus_constant(0, 0)
                for n in units(t, 6, tern):
                    ternary(n)
                if up:
                    hidden_sum(g, j, 2)
                for n in units(t, 7, tern):
                    ternary(n)

            nc.gpsimd.memset(ident[:, :], 0.0).then_inc(zeros_ready, 1)
            pool.wait_ge(zeros_ready, 1)
            nc.gpsimd.affine_select(out=ident[:, :], in_=ident[:, :], compare_op=ALU.not_equal, fill=1.0, base=0,
                                    pattern=[[-1, P]], channel_multiplier=1).then_inc(ident_ready, 1)
            pool.wait_ge(ident_ready, 1)
            nc.gpsimd.tensor_scalar(ident_b[:, :], ident[:, :], 1.0, 1.0, ALU.mult, ALU.mult).then_inc(consts_ready, 1)
            x_norm(0, 0)
            pool.wait_ge(small_in, 16 * 7)
            nc.gpsimd.tensor_tensor(qk_norm[:, :], qk_norm[:, :], nk_in[:, :], ALU.mult).then_inc(norms_ready, 1)
            q_norm(0)
            k_rms_of(0)
            x_norm(1, 1)
            for j in range(J):
                slot(0, j, True, j >= 2, False)
            with pool.Fori(1, NG - 1) as g:
                for j in range(J):
                    slot(g, j, False, True, True)
            for j in range(J):
                slot(NG - 1, j, False, True, True)
            hidden_sum(NG - 1, J - 1, 3)
            x1_norm(NT - 1, J - 1)
            hidden_gain(NG, 0)
            for j in range(2):
                for f in range(UP):
                    hidden_sum(NG, j, f)
            hidden_gain(NG, 2)


def kernel(x, ctx_2048, g_xattn, g_ffn, L0_xattn_q_w, L0_xattn_q_b, L0_xattn_k_w, L0_xattn_k_b, L0_xattn_v_w,
           L0_xattn_v_b, L0_xattn_k_img_w, L0_xattn_k_img_b, L0_xattn_v_img_w, L0_xattn_v_img_b, L0_xattn_o_w,
           L0_xattn_o_b, L0_xattn_norm_q_w, L0_xattn_norm_k_w, L0_xattn_norm_k_img_w, L0_ffn_W_fc, L0_ffn_W_proj):
    import numpy as np
    import concourse.bacc as bacc
    from concourse.bass_utils import run_bass_kernel_spmd

    def chunks(w_t):
        return np.ascontiguousarray(w_t.reshape(-1, P, w_t.shape[1]).transpose(1, 0, 2))

    def rows(v):
        return np.ascontiguousarray(np.broadcast_to(np.asarray(v).reshape(1, -1), (P, np.asarray(v).size)))

    x = np.asarray(x)
    c = np.asarray(ctx_2048)
    nt, s, d = c.shape
    ctx_t = np.ascontiguousarray(c.reshape(nt, s, d // P, P).transpose(0, 3, 2, 1)).reshape(nt, P, d // P * s)
    flat = lambda w: chunks(np.asarray(w).T).reshape(P, -1)
    ins = {
        "x": np.ascontiguousarray(x), "ctx_t": ctx_t,
        "gains": rows(np.concatenate([np.asarray(g_xattn)[0:1], np.asarray(g_ffn)[0:1]])),
        "wq_t": flat(L0_xattn_q_w), "wk_t": flat(L0_xattn_k_img_w), "wv_t": flat(L0_xattn_v_img_w),
        "wo_t": flat(L0_xattn_o_w),
        "q_b": rows(L0_xattn_q_b), "k_b": rows(L0_xattn_k_img_b), "o_b": rows(L0_xattn_o_b),
        "norm_q": rows(L0_xattn_norm_q_w), "norm_k": rows(L0_xattn_norm_k_img_w),
        "v_b": np.ascontiguousarray(np.asarray(L0_xattn_v_img_b).reshape(d // P, P).T),
        "w_fc_t": chunks(np.asarray(L0_ffn_W_fc).T), "w_proj_t": chunks(np.asarray(L0_ffn_W_proj).T),
    }
    nc = bacc.Bacc("TRN2", target_bir_lowering=False, num_devices=1)
    args = {n: nc.dram_tensor(f"in_{n}", a.shape, mybir.dt.from_np(a.dtype), kind="ExternalInput").ap()
            for n, a in ins.items()}
    out = nc.dram_tensor("out", x.shape, F32, kind="ExternalOutput").ap()
    gated_cross_attention_kernel(nc, out=out, **args)
    got = run_bass_kernel_spmd(nc, [{f"in_{n}": a for n, a in ins.items()}], core_ids=[0])
    return got.results[0]["out"]
```
